# Optimizing a Trainium2 kernel written in Bass

```python
import numpy as np
import jax
import jax.numpy as jnp

def _softmax(x, axis=-1):
    return jax.nn.softmax(x, axis=axis)

def _gelu(x):
    return jax.nn.gelu(x, approximate=True)

def _silu(x):
    return jax.nn.silu(x)

def _sigmoid(x):
    return jax.nn.sigmoid(x)

def _layernorm(x, axis=-1, eps=1e-05):
    m = jnp.mean(x, axis=axis, keepdims=True)
    v = jnp.var(x, axis=axis, keepdims=True)
    return (x - m) / jnp.sqrt(v + eps)

def _scatter_add(tgt, idx, src, axis=0):
    return tgt.at[idx].add(src)

def _segment_sum(src, seg, n):
    return jax.ops.segment_sum(src, seg, n)
kernel_name = 'mk_seq_postln_d1_jaxref_r4_a786d5'

def setup_inputs(seed: int=0):
    np.random.seed(seed)
    _w = jnp.asarray

    def _L0_attn_setup():
        import jax, jax.numpy as jnp
        import numpy as np
        B, N, E, H = (2, 512, 256, 16)
        D = E // H
        LN_EPS = 1e-05
        key = jax.random.key(seed)
        k1, k2 = jax.random.split(key)
        x = jax.random.normal(k1, (B, N, E), dtype=jnp.float32)
        gamma = jnp.ones((E,), dtype=jnp.float32)
        beta = jnp.zeros((E,), dtype=jnp.float32)
        w_qkv = jax.random.normal(k2, (3 * E, E), dtype=jnp.float32) * E ** (-0.5)
        return {'x': x, 'gamma': gamma, 'beta': beta, 'w_qkv': w_qkv}
    _L0_attn_in = _L0_attn_setup()

    def _L0_ffn_setup():
        import jax, jax.numpy as jnp
        import numpy as np
        D_IN, D_HID = (256, 1024)

        def _ternary(key, shape):
            return jax.random.randint(key, shape, -1, 2).astype(jnp.float32)

        def _tlin(x, w, s):
            return jnp.einsum('bsi,oi->bso', x, w) * s
        key = jax.random.key(seed)
        ks = jax.random.split(key, 12)
        inv = lambda fan: 1.0 / np.sqrt(fan).astype(np.float32)
        return {'x': jax.random.normal(ks[0], (4, 512, D_IN), dtype=jnp.float32), 'w1_w': _ternary(ks[1], (D_HID, D_IN)), 'w1_s': jax.random.uniform(ks[2], (D_HID,), dtype=jnp.float32) * inv(D_IN), 'w2_w': _ternary(ks[3], (D_HID, D_IN)), 'w2_s': jax.random.uniform(ks[4], (D_HID,), dtype=jnp.float32) * inv(D_IN), 'h1_w': _ternary(ks[5], (D_HID, D_HID)), 'h1_s': jax.random.uniform(ks[6], (D_HID,), dtype=jnp.float32) * inv(D_HID), 'h2_w': _ternary(ks[7], (D_HID, D_HID)), 'h2_s': jax.random.uniform(ks[8], (D_HID,), dtype=jnp.float32) * inv(D_HID), 'w3_w': _ternary(ks[9], (D_IN, D_HID)), 'w3_s': jax.random.uniform(ks[10], (D_IN,), dtype=jnp.float32) * inv(D_HID)}
    _L0_ffn_in = _L0_ffn_setup()
    _d = {'L0_attn_x': _L0_attn_in['x'], 'L0_attn_gamma': _L0_attn_in['gamma'], 'L0_attn_beta': _L0_attn_in['beta'], 'L0_attn_w_qkv': _L0_attn_in['w_qkv'], 'L0_ffn_w1_w': _L0_ffn_in['w1_w'], 'L0_ffn_w1_s': _L0_ffn_in['w1_s'], 'L0_ffn_w2_w': _L0_ffn_in['w2_w'], 'L0_ffn_w2_s': _L0_ffn_in['w2_s'], 'L0_ffn_h1_w': _L0_ffn_in['h1_w'], 'L0_ffn_h1_s': _L0_ffn_in['h1_s'], 'L0_ffn_h2_w': _L0_ffn_in['h2_w'], 'L0_ffn_h2_s': _L0_ffn_in['h2_s'], 'L0_ffn_w3_w': _L0_ffn_in['w3_w'], 'L0_ffn_w3_s': _L0_ffn_in['w3_s']}
    _x0 = _d['L0_attn_x']
    _d['L0_attn_x'] = jax.random.normal(jax.random.fold_in(jax.random.key(seed), 1), (1, 4096, 256), dtype=_x0.dtype)
    del _x0
    return _d

def reference(L0_attn_x, L0_attn_gamma, L0_attn_beta, L0_attn_w_qkv, L0_ffn_w1_w, L0_ffn_w1_s, L0_ffn_w2_w, L0_ffn_w2_s, L0_ffn_h1_w, L0_ffn_h1_s, L0_ffn_h2_w, L0_ffn_h2_s, L0_ffn_w3_w, L0_ffn_w3_s):

    def _L0_attn_ref(x, gamma, beta, w_qkv):
        import jax, jax.numpy as jnp
        import numpy as np
        B, N, E, H = (2, 512, 256, 16)
        D = E // H
        LN_EPS = 1e-05
        b, n, e = x.shape
        h, d = (H, E // H)
        mu = jnp.mean(x, axis=-1, keepdims=True)
        var = jnp.mean(jnp.square(x - mu), axis=-1, keepdims=True)
        xn = (x - mu) * jax.lax.rsqrt(var + LN_EPS) * gamma + beta
        qkv = jnp.einsum('bne,fe->bnf', xn, w_qkv)
        q, k, v = jnp.split(qkv, 3, axis=-1)

        def to_heads(t):
            return t.reshape(b, n, h, d).transpose(0, 2, 1, 3)
        q = to_heads(q) * d ** (-0.5)
        k = to_heads(k)
        v = to_heads(v)
        sim = jnp.einsum('bhqd,bhkd->bhqk', q, k)
        causal_mask = jnp.triu(jnp.ones((n, n), dtype=bool), k=1)
        neg = -jnp.finfo(sim.dtype).max
        sim = jnp.where(causal_mask, neg, sim)
        attn = jax.nn.softmax(sim, axis=-1)
        out = jnp.einsum('bhqk,bhkd->bhqd', attn, v)
        return out.transpose(0, 2, 1, 3).reshape(b, n, h * d)

    def _L0_ffn_ref(x, w1_w, w1_s, w2_w, w2_s, h1_w, h1_s, h2_w, h2_s, w3_w, w3_s):
        import jax, jax.numpy as jnp
        import numpy as np
        D_IN, D_HID = (256, 1024)

        def _ternary(key, shape):
            return jax.random.randint(key, shape, -1, 2).astype(jnp.float32)

        def _tlin(x, w, s):
            return jnp.einsum('bsi,oi->bso', x, w) * s
        h = jax.nn.silu(_tlin(x, w1_w, w1_s)) * _tlin(x, w2_w, w2_s)
        h = jax.nn.gelu(_tlin(h, h1_w, h1_s), approximate=False)
        h = jax.nn.gelu(_tlin(h, h2_w, h2_s), approximate=False)
        return _tlin(h, w3_w, w3_s)
    x = L0_attn_x
    x = _layernorm(x + _L0_attn_ref(x, L0_attn_gamma, L0_attn_beta, L0_attn_w_qkv), axis=-1)
    x = _layernorm(x + _L0_ffn_ref(x, L0_ffn_w1_w, L0_ffn_w1_s, L0_ffn_w2_w, L0_ffn_w2_s, L0_ffn_h1_w, L0_ffn_h1_s, L0_ffn_h2_w, L0_ffn_h2_s, L0_ffn_w3_w, L0_ffn_w3_s), axis=-1)
    return x

_drawn_inputs = setup_inputs


def setup_inputs(seed=0):
    import zlib

    import numpy as np

    out = dict(_drawn_inputs(seed))
    spreads = {'L0_attn_gamma': (1.0, 0.2), 'L0_attn_beta': (0.0, 0.1)}
    factors = {'L0_ffn_w1_w': 8.0,
     'L0_ffn_w1_s': 8.0,
     'L0_ffn_w2_w': 8.0,
     'L0_ffn_w2_s': 8.0,
     'L0_ffn_h1_w': 8.0,
     'L0_ffn_h1_s': 8.0,
     'L0_ffn_h2_w': 8.0,
     'L0_ffn_h2_s': 8.0,
     'L0_ffn_w3_w': 8.0,
     'L0_ffn_w3_s': 8.0}
    for name, (base, spread) in spreads.items():
        noise = np.random.default_rng([zlib.crc32(name.encode()), seed]).standard_normal(out[name].shape)
        drawn = base * np.exp(spread * noise) if base else spread * noise
        out[name] = jnp.asarray(drawn.astype(out[name].dtype))
    for name, factor in factors.items():
        out[name] = (out[name] * factor).astype(out[name].dtype)
    return out
```

```python
import concourse.bass as bass
from concourse import mybir
from contextlib import ExitStack

fp32 = mybir.dt.float32
fp32r = mybir.dt.float32r
bf16 = mybir.dt.bfloat16
ALU = mybir.AluOpType
ACT = mybir.ActivationFunctionType
AX = mybir.AxisListType

S, E, H, FF = 4096, 256, 16, 1024
D = E // H
P = 128
EC, FC = E // P, FF // P
QB = 512
NJ = S // QB
TI = QB // P
G, GH = 4, 4
GE = GH * D
EPS = 1e-5
MASK = -1e30
VW = 32
ROWS = 4 * D
ROWSM = ROWS + 2
NST, NMX, NPB = 4, 2, 2
NQ = 4


def tiles_of(j):
    return TI * (j + 1)


TBASE = [sum(tiles_of(i) for i in range(j)) for j in range(NJ + 1)]
NT = TBASE[NJ]
MBASE = [sum(GH * TI * (i + 1) for i in range(j)) for j in range(NJ + 1)]
NM = MBASE[NJ]


def max_unit(j, n):
    h, rest = divmod(n, TI * (j + 1))
    i, c = divmod(rest, j + 1)
    return h, i, c, QB if c < j else P * (i + 1)


def attention_steps():
    ahead = [(j, n) for j in range(1, NJ) for n in range(MBASE[j + 1] - MBASE[j])]
    plan, at = {}, 0
    for j in range(NJ):
        T = tiles_of(j)
        goal = min(len(ahead), sum(1 for b, _ in ahead if b <= j + 1) + LEAD[j])
        begin, stop = at, T - 1 if T > 4 else T
        for t in range(T):
            upto = begin + (goal - begin) * min(t + 1, stop) // stop
            plan[j, t] = ahead[at:upto]
            at = upto
    assert at == len(ahead)
    return plan


LEAD = [0, 8, 12, 16, 20, 24, 0, 0]
PLAN = attention_steps()
LAST_UNIT = [MBASE[j + 1] - MBASE[j] - 1 for j in range(NJ)]
PREP = {(j, 1): j + 2 for j in range(NJ - 2)}


def misc_uses():
    uses = []
    for j in range(NJ):
        for t in range(tiles_of(j)):
            if t == 0 and j > 0:
                uses.append(("acc", j - 1))
            if (j, t) in PREP:
                uses += [("qk", PREP[j, t]), ("v", PREP[j, t])]
            uses += [("max", b) for b, n in PLAN[j, t] if n == LAST_UNIT[b]]
    return uses + [("acc", NJ - 1)]


MISC_USES = [("qk", 0), ("v", 0), ("qk", 1), ("v", 1), ("max", 0)] + misc_uses()


def block_kernel(nc, x, gamma, beta, wqkv, w1, s1, w2, s2, h1w, h1s, h2w, h2s, w3, s3, out):
    with ExitStack() as ctx:
        def sb(name, shape, dt=fp32):
            return ctx.enter_context(nc.sbuf_tensor(name, shape, dt))

        xres = sb("xres", [P, S // P, E])
        ident = sb("ident", [P, P])
        eps = sb("eps", [P, 1])
        banks = [ctx.enter_context(nc.psum_tensor(f"bank{i}", [P, 512], fp32)) for i in range(8)]
        with ExitStack() as own:
            def sba(name, shape, dt=fp32):
                return own.enter_context(nc.sbuf_tensor(name, shape, dt))

            xnT = sba("xnT", [P, EC, S])
            KS = sba("KS", [ROWSM, GH, S], fp32r)
            V = sba("V", [P, S // P, GH, VW])
            qscale = sba("qscale", [P, 1])
            mask = sba("mask", [P, P], bf16)
            ident16 = sba("ident16", [P, P], bf16)
            normalise(nc, x, gamma, beta, xres, ident, eps, xnT, KS, V, qscale, mask, ident16, banks)
            attend(nc, wqkv, xres, ident, xnT, KS, V, qscale, mask, ident16, banks)
        feed_forward(nc, w1, s1, w2, s2, h1w, h1s, h2w, h2s, w3, s3, out, xres, ident, eps, banks)


def clear(nc, sems):
    for s in sems:
        nc.gpsimd.sem_clear(s)
    nc.all_engine_barrier()


def normalise(nc, x, gamma, beta, xres, ident, eps, xnT, KS, V, qscale, mask, ident16, banks):
    with ExitStack() as ctx:
        def sem(name):
            return ctx.enter_context(nc.semaphore(name))

        def sb(name, shape, dt=fp32):
            return ctx.enter_context(nc.sbuf_tensor(name, shape, dt))

        xn = sb("xn", [P, 2, TI, E])
        gb = sb("gb", [P, 2, EC])
        stats = sb("stats", [P, TI, 6])
        mv = sb("mv", [P, TI, 2])
        std = sb("std", [P, TI, 1])
        rstd = sb("rstd", [P, TI, 1])

        const_load = sem("const_load")
        x_load = [sem(f"x_load{c}") for c in range(NJ)]
        zeroed = sem("zeroed")
        consts = sem("consts")
        cast_done = sem("cast_done")
        stat_done = sem("stat_done")
        std_done = sem("std_done")
        rstd_done = sem("rstd_done")
        xn_done = sem("xn_done")
        xnt_ready = sem("xnt_ready")
        xnt_done = sem("xnt_done")
        block = ctx.enter_context(nc.Block())

        @block.sync
        def _(sp):
            sp.dma_start(gb[:, 0, :], gamma).then_inc(const_load, 16)
            sp.dma_start(gb[:, 1, :], beta).then_inc(const_load, 16)
            for c in range(NJ):
                sp.dma_start(xres[:, TI * c:TI * (c + 1), :],
                             x[0, QB * c:QB * (c + 1), :].rearrange("(t p) e -> p t e", p=P)).then_inc(x_load[c], 16)

        @block.gpsimd
        def _(pool):
            pool.memset(ident[:, :], 0.0).then_inc(zeroed, 1)
            pool.memset(mask[:, :], 0.0).then_inc(zeroed, 1)
            pool.memset(eps[:, :], EPS).then_inc(consts, 1)
            pool.memset(qscale[:, :], float(D) ** -0.5).then_inc(zeroed, 1)
            pool.wait_ge(zeroed, 3)
            pool.affine_select(out=ident[:, :], in_=ident[:, :], compare_op=ALU.not_equal, fill=1.0, base=0,
                               pattern=[[-1, P]], channel_multiplier=1).then_inc(consts, 1)
            pool.affine_select(out=mask[:, :], in_=mask[:, :], compare_op=ALU.is_ge, fill=MASK, base=0,
                               pattern=[[-1, P]], channel_multiplier=1).then_inc(consts, 1)
            pool.affine_select(out=qscale[:, :], in_=qscale[:, :], compare_op=ALU.is_gt, fill=1.0, base=GE,
                               pattern=[[0, 1]], channel_multiplier=-1).then_inc(consts, 1)
            pool.memset(V[:, :, :, :], 0.0).then_inc(zeroed, 1)
            pool.wait_ge(zeroed, 4)
            pool.memset(V[:, :, :, D:D + 1], 1.0).then_inc(consts, 1)
            pool.wait_ge(consts, 5)
            pool.memset(KS[ROWS:ROWSM, :, :].bitcast(fp32), 1.0).then_inc(consts, 1)

        @block.scalar
        def _(act):
            act.wait_ge(const_load, 32)

            def deviation(c):
                act.wait_ge(stat_done, 2 * TI * (c + 1))
                act.activation(std[:, :, :], mv[:, :, 1:2], ACT.Sqrt, bias=eps[:, :]).then_inc(std_done, 1)

            act.wait_ge(consts, 6)
            deviation(0)
            for c in range(NJ):
                if c < NJ - 1:
                    deviation(c + 1)
                for f in range(EC):
                    act.wait_ge(xnt_ready, EC * c + f + 1)
                    act.activation(xnT[:, f, QB * c:QB * (c + 1)], banks[(EC * c + f) % 4][:, :], ACT.Identity,
                                   scale=gb[:, 0, f:f + 1], bias=gb[:, 1, f:f + 1]).then_inc(xnt_done, 1)

        @block.vector
        def _(dve):
            for c in range(NJ):
                base = 2 * TI * c
                dve.wait_ge(x_load[c], 16)
                for i in range(TI):
                    dve.bn_stats(stats[:, i, :], xres[:, TI * c + i, :]).then_inc(stat_done, 1)
                dve.wait_ge(stat_done, base + TI)
                for i in range(TI):
                    dve.bn_aggr(mv[:, i, :], stats[:, i, :]).then_inc(stat_done, 1)
                dve.wait_ge(std_done, c + 1)
                dve.reciprocal(rstd[:, :, :], std[:, :, :]).then_inc(rstd_done, 1)
                dve.wait_ge(rstd_done, c + 1)
                if c >= 2:
                    dve.wait_ge(xnt_ready, EC * (c - 1))
                for i in range(TI):
                    dve.tensor_scalar(xn[:, c % 2, i, :], xres[:, TI * c + i, :], mv[:, i, 0:1], rstd[:, i, :],
                                      ALU.subtract, ALU.mult).then_inc(xn_done, 1)
            dve.wait_ge(consts, 6)
            dve.tensor_copy(ident16[:, :], ident[:, :]).then_inc(cast_done, 1)

        @block.tensor
        def _(pe):
            pe.wait_ge(consts, 6)
            for c in range(NJ):
                pe.wait_ge(xn_done, TI * (c + 1))
                for f in range(EC):
                    n = EC * c + f
                    if n >= 4:
                        pe.wait_ge(xnt_done, n - 3)
                    for i in range(TI):
                        last = pe.transpose(banks[n % 4][:, P * i:P * (i + 1)],
                                            xn[:, c % 2, i, P * f:P * (f + 1)], ident[:, :])
                    last.then_inc(xnt_ready, 1)


def attend(nc, wqkv, xres, ident, xnT, KS, V, qscale, mask, ident16, banks):
    with ExitStack() as ctx:
        sems = []

        def sem(name):
            sems.append(ctx.enter_context(nc.semaphore(name)))
            return sems[-1]

        def sb(name, shape, dt=fp32):
            return ctx.enter_context(nc.sbuf_tensor(name, shape, dt))

        QS = sb("QS", [ROWSM, NQ, GH, QB], fp32r)
        PR = sb("PR", [P, NPB, GH, QB])
        wg = sb("wg", [P, EC, 3 * GE])
        qk_hi = sb("qk_hi", [P, QB], fp32r)
        qk_lo = sb("qk_lo", [P, QB], fp32r)
        acc_sb = sb("acc_sb", [P, QB])
        pm = sb("pm", [P, GH * TI, NJ])
        rowmax = sb("rowmax", [P, GH * TI])
        mneg = sb("mneg", [P, 2, GH * TI], fp32r)
        mrow = sb("mrow", [2 * GH * TI, P], fp32r)
        recip = sb("recip", [P, TI, GH, 1])
        attn = sb("attn", [P, TI, GH, D])

        ST, MX, ACC, MISC = banks[0:NST], banks[4:6], banks[6], banks[7]

        wg_load = sem("wg_load")
        qk_ready = sem("qk_ready")
        hi_done = sem("hi_done")
        lo_done = sem("lo_done")
        stacked = sem("stacked")
        v_ready = sem("v_ready")
        v_done = sem("v_done")
        mx_ready = sem("mx_ready")
        mx_done = sem("mx_done")
        rowmax_done = sem("rowmax_done")
        mneg_hi = sem("mneg_hi")
        mneg_done = sem("mneg_done")
        mt_ready = sem("mt_ready")
        mrow_done = sem("mrow_done")
        max_stacked = sem("max_stacked")
        st_ready = sem("st_ready")
        exp_done = sem("exp_done")
        masked = sem("masked")
        av_done = sem("av_done")
        acc_done = sem("acc_done")
        at_ready = sem("at_ready")
        recip_done = sem("recip_done")
        attn_done = sem("attn_done")
        res_done = sem("res_done")

        def st_count(j, t, h):
            return GH * (TBASE[j] + t) + h + 1

        def tile_count(j, t):
            return TBASE[j] + t + 1

        def stages(j, t):
            return PREP.get((j, t)), PLAN[j, t]

        def program(g):
            block = ctx_g.enter_context(nc.Block())

            @block.sync
            def _(sp):
                sp.dma_start(wg[:, :, :], wqkv[bass.ds(g, 1), :, :].rearrange("o p (c f) -> p (o c) f", c=EC))\
                  .then_inc(wg_load, 16)

                def stack(j, part, rows_q, rows_k):
                    for r in rows_q:
                        for h in range(GH):
                            sp.dma_start(QS[r * D:(r + 1) * D, j % NQ, h, :].bitcast(fp32),
                                         part[h * D:(h + 1) * D, :].bitcast(fp32)).then_inc(stacked, 16)
                    for r in rows_k:
                        for h in range(GH):
                            sp.dma_start(KS[r * D:(r + 1) * D, h, QB * j:QB * (j + 1)].bitcast(fp32),
                                         part[GE + h * D:GE + (h + 1) * D, :].bitcast(fp32)).then_inc(stacked, 16)

                def stack_block(j):
                    sp.wait_ge(hi_done, j + 1)
                    stack(j, qk_hi, (0, 2), (0, 1))
                    sp.wait_ge(lo_done, j + 1)
                    stack(j, qk_lo, (1, 3), (2, 3))

                def stack_max(j):
                    sp.wait_ge(mrow_done, j + 1)
                    for part in range(2):
                        sp.dma_start(QS[ROWS + part:ROWS + part + 1, j % NQ, :, :].bitcast(fp32),
                                     mrow[part * GH * TI:(part + 1) * GH * TI, :].bitcast(fp32)).then_inc(max_stacked, 16)

                stack_block(0)
                stack_block(1)
                stack_max(0)
                for j in range(NJ):
                    for t in range(tiles_of(j)):
                        prepared, units = stages(j, t)
                        if prepared:
                            stack_block(prepared)
                        for b, n in units:
                            if n == LAST_UNIT[b]:
                                stack_max(b)

            @block.gpsimd
            def _(pool):
                for j in range(NJ):
                    for i in range(TI):
                        t = TI * j + i
                        pool.wait_ge(exp_done, st_count(j, t, GH - 1))
                        diag = PR[:, t % NPB, :, P * i:P * (i + 1)]
                        pool.affine_select(out=diag, in_=diag, compare_op=ALU.is_ge, fill=0.0, base=0,
                                           pattern=[[0, GH], [1, P]], channel_multiplier=-1).then_inc(masked, 1)

            @block.scalar
            def _(act):
                def prepare(j):
                    act.wait_ge(qk_ready, j + 1)
                    if j >= 1:
                        act.wait_ge(stacked, 16 * 32 * j)
                    act.activation(qk_hi[:, :], MISC[:, :], ACT.Copy, scale=qscale[:, :]).then_inc(hi_done, 1)
                    act.wait_ge(v_ready, j + 1)
                    act.activation(V[:, TI * j:TI * (j + 1), :, 0:D],
                                   MISC[:, 0:TI * GE].rearrange("p (i h d) -> p i h d", i=TI, h=GH),
                                   ACT.Copy).then_inc(v_done, 1)

                def copy_max(j):
                    act.wait_ge(mt_ready, j + 1)
                    if j >= 1:
                        act.wait_ge(max_stacked, 32 * j)
                    act.activation(mrow[:, :], MISC[0:2 * GH * TI, 0:P], ACT.Copy).then_inc(mrow_done, 1)

                def copy_acc(j):
                    act.wait_ge(av_done, tile_count(j, tiles_of(j) - 1))
                    if j >= 1:
                        act.wait_ge(at_ready, j)
                    act.activation(acc_sb[:, :], ACC[:, :], ACT.Copy).then_inc(acc_done, 1)

                prepare(0)
                prepare(1)
                copy_max(0)
                for j in range(NJ):
                    for t in range(tiles_of(j)):
                        prepared, units = stages(j, t)
                        off = max(0, P * (t - TI * j))
                        for h in range(GH):
                            act.wait_ge(st_ready, st_count(j, t, h))
                            if h == 0 and tile_count(j, t) > NPB:
                                act.wait_ge(av_done, tile_count(j, t) - NPB)
                            act.activation(PR[:, t % NPB, h, off:QB], ST[h][:, off:QB], ACT.Exp).then_inc(exp_done, 1)
                        if prepared:
                            prepare(prepared)
                        for b, n in units:
                            if n == LAST_UNIT[b]:
                                copy_max(b)
                    copy_acc(j)

            @block.vector
            def _(dve):
                def split(j):
                    dve.wait_ge(hi_done, j + 1)
                    if j >= 1:
                        dve.wait_ge(stacked, 16 * 32 * j)
                    dve.scalar_tensor_tensor(out=qk_lo[:, :], in0=MISC[:, :], scalar=qscale[:, :],
                                             in1=qk_hi[:, :].bitcast(fp32), op0=ALU.mult, op1=ALU.subtract)\
                       .then_inc(lo_done, 1)

                def maximum(j, n):
                    h, i, c, width = max_unit(j, n)
                    v = MBASE[j] + n
                    dve.wait_ge(mx_ready, v + 1)
                    dve.reduce_max(pm[:, h * TI + i, c:c + 1], MX[v % NMX][:, 0:width], AX.X).then_inc(mx_done, 1)

                def row_maximum(j):
                    dve.wait_ge(mx_done, MBASE[j + 1])
                    dve.tensor_reduce(rowmax[:, :], pm[:, :, 0:j + 1], axis=AX.X, op=ALU.max).then_inc(rowmax_done, 1)
                    dve.wait_ge(rowmax_done, j + 1)
                    if j >= 1:
                        dve.wait_ge(mt_ready, j)
                    dve.tensor_scalar(mneg[:, 0, :], rowmax[:, :], -1.0, None, ALU.mult).then_inc(mneg_hi, 1)
                    dve.wait_ge(mneg_hi, j + 1)
                    dve.scalar_tensor_tensor(out=mneg[:, 1, :], in0=rowmax[:, :], scalar=-1.0,
                                             in1=mneg[:, 0, :].bitcast(fp32), op0=ALU.mult, op1=ALU.subtract)\
                       .then_inc(mneg_done, 1)

                def attention_out(j):
                    dve.wait_ge(at_ready, j + 1)
                    sums = MISC[:, :].rearrange("p (i h w) -> p i h w", i=TI, h=GH)
                    dve.reciprocal(recip[:, :, :, :], sums[:, :, :, D:D + 1]).then_inc(recip_done, 1)
                    dve.wait_ge(recip_done, j + 1)
                    dve.tensor_tensor(attn[:, :, :, :], sums[:, :, :, 0:D],
                                      recip[:, :, :, :].broadcast_to([P, TI, GH, D]), ALU.mult).then_inc(attn_done, 1)
                    dve.wait_ge(attn_done, j + 1)
                    own = xres[:, TI * j:TI * (j + 1), bass.ds(g * GE, GE)]
                    dve.tensor_tensor(own, own, attn[:, :, :, :].rearrange("p i h d -> p i (h d)"), ALU.add)\
                       .then_inc(res_done, 1)

                split(0)
                split(1)
                for n in range(LAST_UNIT[0] + 1):
                    maximum(0, n)
                row_maximum(0)
                for j in range(NJ):
                    for t in range(tiles_of(j)):
                        prepared, units = stages(j, t)
                        for b, n in units:
                            maximum(b, n)
                            if n == LAST_UNIT[b]:
                                row_maximum(b)
                        if t == 0 and j > 0:
                            attention_out(j - 1)
                        if prepared:
                            split(prepared)
                attention_out(NJ - 1)

            @block.tensor
            def _(pe):
                def misc_free(kind, j):
                    at = MISC_USES.index((kind, j))
                    if at == 0:
                        return
                    kind, j = MISC_USES[at - 1]
                    if kind == "qk":
                        pe.wait_ge(lo_done, j + 1)
                    if kind == "v":
                        pe.wait_ge(v_done, j + 1)
                    if kind == "max":
                        pe.wait_ge(mrow_done, j + 1)
                    if kind == "acc":
                        pe.wait_ge(attn_done, j + 1)

                def project(j):
                    misc_free("qk", j)
                    for c in range(EC):
                        last = pe.matmul(MISC[:, :], wg[:, c, 0:2 * GE], xnT[:, c, QB * j:QB * (j + 1)],
                                         start=(c == 0), stop=(c == EC - 1))
                    last.then_inc(qk_ready, 1)
                    misc_free("v", j)
                    for i in range(TI):
                        at = QB * j + P * i
                        for c in range(EC):
                            last = pe.matmul(MISC[:, GE * i:GE * (i + 1)], xnT[:, c, at:at + P],
                                             wg[:, c, 2 * GE:3 * GE], start=(c == 0), stop=(c == EC - 1))
                    last.then_inc(v_ready, 1)

                def maximum(j, n):
                    h, i, c, width = max_unit(j, n)
                    v = MBASE[j] + n
                    if n == 0:
                        pe.wait_ge(stacked, 16 * 32 * (j + 1))
                    if v >= NMX:
                        pe.wait_ge(mx_done, v - NMX + 1)
                    diagonal = c == j
                    last = pe.matmul(MX[v % NMX][:, 0:width], QS[0:ROWS, j % NQ, h, P * i:P * (i + 1)],
                                     KS[0:ROWS, h, QB * c:QB * c + width], start=True, stop=not diagonal)
                    if diagonal:
                        last = pe.matmul(MX[v % NMX][:, width - P:width], ident16[:, :], mask[:, :],
                                         start=False, stop=True)
                    last.then_inc(mx_ready, 1)

                def transpose_max(j):
                    misc_free("max", j)
                    pe.wait_ge(mneg_done, j + 1)
                    pe.transpose(MISC[0:2 * GH * TI, 0:P], mneg[:, :, :].rearrange("p a n -> p (a n)").bitcast(fp32),
                                 ident[:, :]).then_inc(mt_ready, 1)

                def score(j, t, h):
                    off = max(0, P * (t - TI * j))
                    if t == 0 and h == 0:
                        pe.wait_ge(max_stacked, 32 * (j + 1))
                    if tile_count(j, t) > 1:
                        pe.wait_ge(exp_done, st_count(j, t, h) - NST)
                    pe.matmul(ST[h][:, off:QB], KS[:, h, P * t:P * (t + 1)], QS[:, j % NQ, h, off:QB],
                              start=True, stop=True).then_inc(st_ready, 1)

                def product(j, t):
                    off = max(0, P * (t - TI * j))
                    if t == 0:
                        if j >= 1:
                            pe.wait_ge(acc_done, j)
                        pe.wait_ge(v_done, j + 1)
                    if t >= TI * j:
                        pe.wait_ge(masked, t + 1)
                    pe.wait_ge(exp_done, st_count(j, t, GH - 1))
                    for h in range(GH):
                        last = pe.matmul(ACC[VW * h:VW * (h + 1), off:QB], V[:, t, h, :], PR[:, t % NPB, h, off:QB],
                                         start=(t == 0), stop=(t == tiles_of(j) - 1))
                    last.then_inc(av_done, 1)

                def transpose_acc(j):
                    misc_free("acc", j)
                    pe.wait_ge(acc_done, j + 1)
                    for i in range(TI):
                        last = pe.transpose(MISC[:, P * i:P * (i + 1)], acc_sb[:, P * i:P * (i + 1)], ident[:, :])
                    last.then_inc(at_ready, 1)

                pe.wait_ge(wg_load, 16)
                project(0)
                project(1)
                for n in range(LAST_UNIT[0] + 1):
                    maximum(0, n)
                transpose_max(0)
                for j in range(NJ):
                    for t in range(tiles_of(j)):
                        prepared, units = stages(j, t)
                        for h in range(GH):
                            score(j, t, h)
                            for b, n in units[len(units) * h // GH:len(units) * (h + 1) // GH]:
                                maximum(b, n)
                        if t == 0 and j > 0:
                            transpose_acc(j - 1)
                        if prepared:
                            project(prepared)
                        if t > 0:
                            product(j, t - 1)
                        for b, n in units:
                            if n == LAST_UNIT[b]:
                                transpose_max(b)
                    product(j, tiles_of(j) - 1)
                transpose_acc(NJ - 1)

        with nc.Fori(0, G) as g:
            with ExitStack() as ctx_g:
                program(g)
            clear(nc, sems)


def feed_forward(nc, w1, s1, w2, s2, h1w, h1s, h2w, h2s, w3, s3, out, xres, ident, eps, banks):
    with ExitStack() as ctx:
        sems = []

        def sem(name, kept=False):
            s = ctx.enter_context(nc.semaphore(name))
            if not kept:
                sems.append(s)
            return s

        def sb(name, shape, dt=fp32):
            return ctx.enter_context(nc.sbuf_tensor(name, shape, dt))

        w1_sb = sb("w1_sb", [P, EC, FF])
        w2_sb = sb("w2_sb", [P, EC, FF])
        h1_sb = sb("h1_sb", [P, FC, FF])
        h2_sb = sb("h2_sb", [P, FC, FF])
        w3_sb = sb("w3_sb", [P, FC, E])
        s_sb = sb("s_sb", [P, 4, FC])
        s3_sb = sb("s3_sb", [P, E])
        x1 = sb("x1", [P, 2, TI, E])
        x1T = sb("x1T", [P, 2, EC, QB])
        hid = sb("hid", [P, 3, FC, QB])
        gate = sb("gate", [P, 2, QB])
        stats = sb("ff_stats", [P, TI, 6])
        mv = sb("ff_mv", [P, TI, 2])
        std = sb("ff_std", [P, TI, 1])
        rstd = sb("ff_rstd", [P, TI, 1])
        ystats = sb("y_stats", [P, TI, 6])
        ymv = sb("y_mv", [P, TI, 2])
        ystd = sb("y_std_sb", [P, TI, 1])
        yrstd = sb("y_rstd_sb", [P, TI, 1])
        y = sb("y", [P, 2, TI, E])
        o_sb = sb("o_sb", [P, 2, TI, E])

        NR = 6
        RING, TB = banks[0:NR], banks[6:8]
        NS, NY = 2 * TI, 3 * TI

        w_load = [sem(f"w_load{i}", kept=True) for i in range(5)]
        s_load = sem("s_load", kept=True)
        x1_stat = sem("x1_stat")
        x1_std = sem("x1_std")
        x1_rstd = sem("x1_rstd")
        y_std = sem("y_std")
        y_rstd = sem("y_rstd")
        x1_done = sem("x1_done")
        x1t_ready = sem("x1t_ready")
        x1t_done = sem("x1t_done")
        glu_ready = sem("glu_ready")
        silu_done = sem("silu_done")
        glu_done = sem("glu_done")
        hid_ready = sem("hid_ready")
        gelu_done = sem("gelu_done")
        y_ready = sem("y_ready")
        y_done = sem("y_done")
        y_stat = sem("y_stat")
        o_done = sem("o_done")
        stored = sem("stored")

        def program(b):
            block = ctx_b.enter_context(nc.Block())

            @block.sync
            def _(sp):
                for T in range(2):
                    sp.wait_ge(o_done, T + 1)
                    sp.dma_start(out_v[bass.ds(2 * b + T, 1), :, :, :].rearrange("o p t e -> p (o t) e"),
                                 o_sb[:, T, :, :]).then_inc(stored, 16)
                sp.wait_ge(stored, 32)

            @block.scalar
            def _(act):
                def copy_x1T(T):
                    for f in range(EC):
                        act.wait_ge(x1t_ready, EC * T + f + 1)
                        act.activation(x1T[:, T, f, :], TB[f][:, :], ACT.Copy).then_inc(x1t_done, 1)

                def std_x1(T):
                    act.wait_ge(x1_stat, NS * (T + 1))
                    act.activation(std[:, :, :], mv[:, :, 1:2], ACT.Sqrt, bias=eps[:, :]).then_inc(x1_std, 1)

                def std_y(T):
                    act.wait_ge(y_stat, NY * (T + 1))
                    act.activation(ystd[:, :, :], ymv[:, :, 1:2], ACT.Sqrt, bias=eps[:, :]).then_inc(y_std, 1)

                std_x1(0)
                copy_x1T(0)
                for T in range(2):
                    for o in range(FC):
                        n = FC * T + o
                        act.wait_ge(glu_ready, n + 1)
                        if n >= 2:
                            act.wait_ge(glu_done, n - 1)
                        act.activation(gate[:, n % 2, :], RING[2 * (o % 3)][:, :], ACT.Silu,
                                       scale=s_sb[:, 0, o:o + 1]).then_inc(silu_done, 1)
                    if T == 0:
                        std_x1(1)
                    else:
                        std_y(0)
                    for layer in range(2):
                        for o in range(FC):
                            n = FC * layer + o
                            act.wait_ge(hid_ready, 2 * FC * T + n + 1)
                            if T == 1 and layer == 1 and o == 0:
                                act.wait_ge(y_ready, TI)
                            act.activation(hid[:, layer + 1, o, :], RING[(4 + n) % NR][:, :], ACT.Gelu,
                                           scale=s_sb[:, 2 + layer, o:o + 1]).then_inc(gelu_done, 1)
                    if T == 0:
                        copy_x1T(1)
                    else:
                        std_y(1)

            @block.vector
            def _(dve):
                def layernorm_x1(T):
                    tok = [xres[:, bass.ds(2 * TI * b + TI * T + i, 1), :].rearrange("p o e -> p (o e)")
                           for i in range(TI)]
                    for i in range(TI):
                        dve.bn_stats(stats[:, i, :], tok[i]).then_inc(x1_stat, 1)
                    dve.wait_ge(x1_stat, NS * T + TI)
                    for i in range(TI):
                        dve.bn_aggr(mv[:, i, :], stats[:, i, :]).then_inc(x1_stat, 1)
                    dve.wait_ge(x1_std, T + 1)
                    dve.reciprocal(rstd[:, :, :], std[:, :, :]).then_inc(x1_rstd, 1)
                    dve.wait_ge(x1_rstd, T + 1)
                    for i in range(TI):
                        dve.tensor_scalar(x1[:, T, i, :], tok[i], mv[:, i, 0:1], rstd[:, i, :],
                                          ALU.subtract, ALU.mult).then_inc(x1_done, 1)

                def gated(T):
                    for o in range(FC):
                        n = FC * T + o
                        dve.wait_ge(silu_done, n + 1)
                        dve.scalar_tensor_tensor(out=hid[:, 0, o, :], in0=RING[2 * (o % 3) + 1][:, :],
                                                 scalar=s_sb[:, 1, o:o + 1], in1=gate[:, n % 2, :],
                                                 op0=ALU.mult, op1=ALU.mult).then_inc(glu_done, 1)

                def residual(T):
                    for i in range(TI):
                        dve.wait_ge(y_ready, TI * T + i + 1)
                        dve.tensor_tensor(y[:, T, i, :], RING[2 + i][:, 0:E], s3_sb[:, :], ALU.mult).then_inc(y_done, 1)
                    for i in range(TI):
                        dve.wait_ge(y_done, TI * T + i + 1)
                        dve.tensor_tensor(y[:, T, i, :], y[:, T, i, :], x1[:, T, i, :], ALU.add).then_inc(y_stat, 1)
                    for i in range(TI):
                        dve.wait_ge(y_stat, NY * T + i + 1)
                        dve.bn_stats(ystats[:, i, :], y[:, T, i, :]).then_inc(y_stat, 1)
                    dve.wait_ge(y_stat, NY * T + 2 * TI)
                    for i in range(TI):
                        dve.bn_aggr(ymv[:, i, :], ystats[:, i, :]).then_inc(y_stat, 1)

                def output(T):
                    dve.wait_ge(y_std, T + 1)
                    dve.reciprocal(yrstd[:, :, :], ystd[:, :, :]).then_inc(y_rstd, 1)
                    dve.wait_ge(y_rstd, T + 1)
                    for i in range(TI):
                        last = dve.tensor_scalar(o_sb[:, T, i, :], y[:, T, i, :], ymv[:, i, 0:1], yrstd[:, i, :],
                                                 ALU.subtract, ALU.mult)
                    last.then_inc(o_done, 1)

                layernorm_x1(0)
                gated(0)
                layernorm_x1(1)
                residual(0)
                gated(1)
                output(0)
                residual(1)
                output(1)

            @block.tensor
            def _(pe):
                def transpose_x1(T):
                    pe.wait_ge(x1_done, TI * (T + 1))
                    for f in range(EC):
                        for i in range(TI):
                            last = pe.transpose(TB[f][:, P * i:P * (i + 1)], x1[:, T, i, P * f:P * (f + 1)],
                                                ident[:, :])
                        last.then_inc(x1t_ready, 1)

                transpose_x1(0)
                for T in range(2):
                    pe.wait_ge(x1t_done, EC * (T + 1))
                    for o in range(FC):
                        if T == 1 and o in (1, 2):
                            pe.wait_ge(y_done, 2 * o)
                        if o >= 3:
                            pe.wait_ge(glu_done, FC * T + o - 2)
                        for w, at in ((w1_sb, 0), (w2_sb, 1)):
                            for c in range(EC):
                                last = pe.matmul(RING[2 * (o % 3) + at][:, :], w[:, c, P * o:P * (o + 1)],
                                                 x1T[:, T, c, :], start=(c == 0), stop=(c == EC - 1))
                        last.then_inc(glu_ready, 1)
                    for layer in range(2):
                        w = (h1_sb, h2_sb)[layer]
                        for o in range(FC):
                            n = FC * layer + o
                            if n >= NR:
                                pe.wait_ge(gelu_done, 2 * FC * T + n - NR + 1)
                            for c in range(FC):
                                if layer == 0 and o == 0:
                                    pe.wait_ge(glu_done, FC * T + max(c, NR - 1) + 1)
                                if layer == 1 and o == 0:
                                    pe.wait_ge(gelu_done, 2 * FC * T + c + 1)
                                last = pe.matmul(RING[(4 + n) % NR][:, :], w[:, c, P * o:P * (o + 1)],
                                                 hid[:, layer, c, :], start=(c == 0), stop=(c == FC - 1))
                            last.then_inc(hid_ready, 1)
                    if T == 0:
                        transpose_x1(1)
                    for i in range(TI):
                        for c in range(FC):
                            if i == 0:
                                pe.wait_ge(gelu_done, 2 * FC * T + FC + max(c, TI + 1) + 1)
                            last = pe.matmul(RING[2 + i][:, 0:E], hid[:, 2, c, P * i:P * (i + 1)], w3_sb[:, c, :],
                                             start=(c == 0), stop=(c == FC - 1))
                        last.then_inc(y_ready, 1)

        with ExitStack() as ctx_l:
            block = ctx_l.enter_context(nc.Block())

            @block.sync
            def _(sp):
                for v, s in enumerate((s1, s2, h1s, h2s)):
                    sp.dma_start(s_sb[:, v, :], s).then_inc(s_load, 16)
                sp.dma_start(s3_sb[:, :], s3.rearrange("(o e) -> o e", o=1).broadcast_to([P, E])).then_inc(s_load, 16)
                for n, (dst, src) in enumerate(((w1_sb, w1), (w2_sb, w2), (h1_sb, h1w), (h2_sb, h2w), (w3_sb, w3))):
                    sp.dma_start(dst[:, :, :], src.rearrange("(c p) f -> p c f", p=P)).then_inc(w_load[n], 16)
                sp.wait_ge(s_load, 16 * 5)
                for n in range(5):
                    sp.wait_ge(w_load[n], 16)

        out_v = out.rearrange("o (b t p) e -> b p (o t) e", p=P, t=TI)
        with nc.Fori(0, NJ // 2) as b:
            with ExitStack() as ctx_b:
                program(b)
            clear(nc, sems)


_OUTS = [((1, S, E), "float32")]


def kernel(**inputs):
    import numpy as _np
    import concourse.bacc as _bacc
    from concourse import mybir as _mybir
    from concourse.bass_utils import run_bass_kernel_spmd as _run

    w = _np.asarray(inputs["L0_attn_w_qkv"]).reshape(3, G, GE, EC, P)
    wqkv = _np.ascontiguousarray(w.transpose(1, 4, 3, 0, 2).reshape(G, P, EC * 3 * GE))

    def by_chunk(v):
        return _np.asarray(v).reshape(-1, P).T

    laid = {
        "x": inputs["L0_attn_x"], "gamma": by_chunk(inputs["L0_attn_gamma"]),
        "beta": by_chunk(inputs["L0_attn_beta"]), "wqkv": wqkv,
        "w1": _np.asarray(inputs["L0_ffn_w1_w"]).T, "s1": by_chunk(inputs["L0_ffn_w1_s"]),
        "w2": _np.asarray(inputs["L0_ffn_w2_w"]).T, "s2": by_chunk(inputs["L0_ffn_w2_s"]),
        "h1": _np.asarray(inputs["L0_ffn_h1_w"]).T, "h1s": by_chunk(inputs["L0_ffn_h1_s"]),
        "h2": _np.asarray(inputs["L0_ffn_h2_w"]).T, "h2s": by_chunk(inputs["L0_ffn_h2_s"]),
        "w3": _np.asarray(inputs["L0_ffn_w3_w"]).T, "s3": inputs["L0_ffn_w3_s"],
    }
    nc = _bacc.Bacc("TRN2", target_bir_lowering=False, num_devices=1)
    arrays, args = {}, []
    for name, a in laid.items():
        a = _np.ascontiguousarray(a)
        arrays[f"in_{name}_dram"] = a
        args.append(nc.dram_tensor(f"in_{name}_dram", a.shape, _mybir.dt.from_np(a.dtype), kind="ExternalInput").ap())
    for i, (shape, dtype) in enumerate(_OUTS):
        args.append(nc.dram_tensor(f"out_{i}_dram", shape, _mybir.dt.from_np(_np.dtype(dtype)), kind="ExternalOutput").ap())
    block_kernel(nc, *args)
    r = _run(nc, [arrays], core_ids=[0])
    return r.results[0]["out_0_dram"]
```

```python
import concourse.bass as bass
from concourse import mybir
from contextlib import ExitStack

fp32 = mybir.dt.float32
fp32r = mybir.dt.float32r
bf16 = mybir.dt.bfloat16
int32 = mybir.dt.int32
ALU = mybir.AluOpType
ACT = mybir.ActivationFunctionType
AX = mybir.AxisListType

S, E, H, FF = 4096, 256, 16, 1024
D = E // H
P = 128
EC, FC = E // P, FF // P
QB = 512
NJ = S // QB
TI = QB // P
G, GH = 4, 4
GE = GH * D
LOW_BITS = 12
WC = 2048
EPS = 1e-5
MASK = -1e30
VW = 32
ROWS = 4 * D
MROW = P - 2
NST, NMX, NPB = 3, 3, 2
AV_AFTER = 3
NQ = 4


def tiles_of(j):
    return TI * (j + 1)


TBASE = [sum(tiles_of(i) for i in range(j)) for j in range(NJ + 1)]
NT = TBASE[NJ]


def max_unit(j, n):
    h, rest = divmod(n, TI * (j + 1))
    i, c = divmod(rest, j + 1)
    return h, i, c, QB if c < j else P * (i + 1)


NEXT = NJ


def units_of(J):
    return GH * TI * (J % NJ + 1)


class Plan:

    def __init__(self, steps, preps, maxima, lead):
        self.steps, self.preps, self.maxima = steps, preps, maxima
        self.prep_at = {at: J for J, at in preps.items() if at}
        self.base = {J: sum(units_of(i) for i in maxima if i < J) for J in maxima}
        ahead = [(J, n) for J in maxima for n in range(units_of(J))]
        self.units, at = {}, 0
        for j in steps:
            T = tiles_of(j)
            goal = min(len(ahead), sum(1 for J, _ in ahead if J <= j + 1) + lead[j])
            first = NEXT_MAX_AT if j == NJ - 1 else 0
            begin, stop = at, T - 2 if T > 4 else T
            for t in range(T):
                upto = begin + (goal - begin) * max(0, min(t + 1, stop) - first) // (stop - first)
                self.units[j, t] = ahead[at:upto]
                at = upto
        self.rest = ahead[at:]
        self.misc = [(kind, J) for J in preps if not preps[J] for kind in ("qk", "v")]
        if not steps:
            self.misc += [("max", J) for J in maxima]
        for j in steps:
            for t in range(tiles_of(j)):
                if t == 0 and j > 0:
                    self.misc.append(("acc", j - 1))
                if (j, t) in self.prep_at:
                    self.misc += [("qk", self.prep_at[j, t]), ("v", self.prep_at[j, t])]
                self.misc += [("max", J) for J, n in self.units[j, t] if n == units_of(J) - 1]
        if steps:
            self.misc.append(("acc", NJ - 1))

    def prep_count(self, J):
        return 1 + list(self.preps).index(J)

    def max_count(self, J):
        return 1 + self.maxima.index(J)

    def stages(self, j, t):
        return self.prep_at.get((j, t)), self.units[j, t]


LEAD = [0, 8, 12, 16, 20, 24, 0, 0]
NEXT_MAX_AT = 14
WITHIN = {J: (J - 2, 1) for J in range(2, NJ)}
START = Plan([], {NEXT: None, NEXT + 1: None}, [NEXT], LEAD)
GROUP = Plan(range(NJ), {**WITHIN, NEXT: (NJ - 1, 6), NEXT + 1: (NJ - 1, 10)}, list(range(1, NEXT + 1)), LEAD)
LAST = Plan(range(NJ), WITHIN, list(range(1, NJ)), LEAD)


def block_kernel(nc, x, gamma, beta, wqkv, w1, s1, w2, s2, h1w, h1s, h2w, h2s, w3, s3, out):
    with ExitStack() as ctx:
        def sb(name, shape, dt=fp32):
            return ctx.enter_context(nc.sbuf_tensor(name, shape, dt))

        xres = sb("xres", [P, S // P, E])
        ident = sb("ident", [P, P])
        eps = sb("eps", [P, 1])
        low_bits = sb("low_bits", [1, 1], int32)
        banks = [ctx.enter_context(nc.psum_tensor(f"bank{i}", [P, 512], fp32)) for i in range(8)]
        with ExitStack() as own:
            def sba(name, shape, dt=fp32):
                return own.enter_context(nc.sbuf_tensor(name, shape, dt))

            xnT = sba("xnT", [P, EC, S])
            KS = sba("KS", [P, GH, S], fp32r)
            QS = sba("QS", [P, NQ, GH, QB], fp32r)
            V = sba("V", [P, S // P, GH, VW])
            qscale = sba("qscale", [P, 1])
            mask = sba("mask", [P, P], bf16)
            ident16 = sba("ident16", [P, P], bf16)
            normalise(nc, x, gamma, beta, xres, ident, eps, xnT, KS, QS, V, qscale, mask, ident16, banks)
            attend(nc, wqkv, xres, ident, xnT, KS, QS, V, qscale, mask, ident16, banks,
                   (w1, w2, h1w, h2w, w3), low_bits)
        inexact = nc.values_load(low_bits[0:1, 0:1], min_val=0, max_val=2 ** LOW_BITS - 1)
        with nc.If(inexact == 0):
            nc.all_engine_barrier()
            feed_forward_exact(nc, w1, s1, w2, s2, h1w, h1s, h2w, h2s, w3, s3, out, xres, ident, eps, banks)
        with nc.Else():
            nc.all_engine_barrier()
            feed_forward(nc, w1, s1, w2, s2, h1w, h1s, h2w, h2s, w3, s3, out, xres, ident, eps, banks)


def clear(nc, sems):
    for s in sems:
        nc.gpsimd.sem_clear(s)
    nc.all_engine_barrier()


def normalise(nc, x, gamma, beta, xres, ident, eps, xnT, KS, QS, V, qscale, mask, ident16, banks):
    with ExitStack() as ctx:
        def sem(name):
            return ctx.enter_context(nc.semaphore(name))

        def sb(name, shape, dt=fp32):
            return ctx.enter_context(nc.sbuf_tensor(name, shape, dt))

        xn = sb("xn", [P, 2, TI, E])
        gb = sb("gb", [P, 2, EC])
        stats = sb("stats", [P, TI, 6])
        mv = sb("mv", [P, TI, 2])
        std = sb("std", [P, TI, 1])
        rstd = sb("rstd", [P, TI, 1])

        const_load = sem("const_load")
        x_load = [sem(f"x_load{c}") for c in range(NJ)]
        zeroed = sem("zeroed")
        consts = sem("consts")
        cast_done = sem("cast_done")
        stat_done = sem("stat_done")
        std_done = sem("std_done")
        rstd_done = sem("rstd_done")
        xn_done = sem("xn_done")
        xnt_ready = sem("xnt_ready")
        xnt_done = sem("xnt_done")
        block = ctx.enter_context(nc.Block())

        @block.sync
        def _(sp):
            sp.dma_start(gb[:, 0, :], gamma).then_inc(const_load, 16)
            sp.dma_start(gb[:, 1, :], beta).then_inc(const_load, 16)
            for c in range(NJ):
                sp.dma_start(xres[:, TI * c:TI * (c + 1), :],
                             x[0, QB * c:QB * (c + 1), :].rearrange("(t p) e -> p t e", p=P)).then_inc(x_load[c], 16)

        @block.gpsimd
        def _(pool):
            pool.memset(ident[:, :], 0.0).then_inc(zeroed, 1)
            pool.memset(mask[:, :], 0.0).then_inc(zeroed, 1)
            pool.memset(eps[:, :], EPS).then_inc(consts, 1)
            pool.memset(qscale[:, :], float(D) ** -0.5).then_inc(zeroed, 1)
            pool.wait_ge(zeroed, 3)
            pool.affine_select(out=ident[:, :], in_=ident[:, :], compare_op=ALU.not_equal, fill=1.0, base=0,
                               pattern=[[-1, P]], channel_multiplier=1).then_inc(consts, 1)
            pool.affine_select(out=mask[:, :], in_=mask[:, :], compare_op=ALU.is_ge, fill=MASK, base=0,
                               pattern=[[-1, P]], channel_multiplier=1).then_inc(consts, 1)
            pool.affine_select(out=qscale[:, :], in_=qscale[:, :], compare_op=ALU.is_gt, fill=1.0, base=GE,
                               pattern=[[0, 1]], channel_multiplier=-1).then_inc(consts, 1)
            pool.memset(V[:, :, :, :], 0.0).then_inc(zeroed, 1)
            pool.wait_ge(zeroed, 4)
            pool.memset(V[:, :, :, D:D + 1], 1.0).then_inc(consts, 1)
            pool.wait_ge(consts, 5)
            pool.memset(KS[ROWS:P, :, :].bitcast(fp32), 0.0).then_inc(zeroed, 1)
            pool.wait_ge(zeroed, 5)
            pool.memset(QS[ROWS:P, :, :, :].bitcast(fp32), 0.0).then_inc(zeroed, 1)
            pool.wait_ge(zeroed, 6)
            low = KS[P - 32:P, :, :]
            pool.affine_select(out=low, in_=low.bitcast(fp32), compare_op=ALU.is_gt, fill=1.0, base=MROW - (P - 32),
                               pattern=[[0, GH], [0, S]], channel_multiplier=-1).then_inc(consts, 1)

        @block.scalar
        def _(act):
            act.wait_ge(const_load, 32)

            def deviation(c):
                act.wait_ge(stat_done, 2 * TI * (c + 1))
                act.activation(std[:, :, :], mv[:, :, 1:2], ACT.Sqrt, bias=eps[:, :]).then_inc(std_done, 1)

            act.wait_ge(consts, 1)
            deviation(0)
            for c in range(NJ):
                if c < NJ - 1:
                    deviation(c + 1)
                for f in range(EC):
                    act.wait_ge(xnt_ready, EC * c + f + 1)
                    act.activation(xnT[:, f, QB * c:QB * (c + 1)], banks[(EC * c + f) % 4][:, :], ACT.Identity,
                                   scale=gb[:, 0, f:f + 1], bias=gb[:, 1, f:f + 1]).then_inc(xnt_done, 1)

        @block.vector
        def _(dve):
            for c in range(NJ):
                base = 2 * TI * c
                dve.wait_ge(x_load[c], 16)
                for i in range(TI):
                    dve.bn_stats(stats[:, i, :], xres[:, TI * c + i, :]).then_inc(stat_done, 1)
                dve.wait_ge(stat_done, base + TI)
                for i in range(TI):
                    dve.bn_aggr(mv[:, i, :], stats[:, i, :]).then_inc(stat_done, 1)
                dve.wait_ge(std_done, c + 1)
                dve.reciprocal(rstd[:, :, :], std[:, :, :]).then_inc(rstd_done, 1)
                dve.wait_ge(rstd_done, c + 1)
                if c >= 2:
                    dve.wait_ge(xnt_ready, EC * (c - 1))
                for i in range(TI):
                    dve.tensor_scalar(xn[:, c % 2, i, :], xres[:, TI * c + i, :], mv[:, i, 0:1], rstd[:, i, :],
                                      ALU.subtract, ALU.mult).then_inc(xn_done, 1)
            dve.wait_ge(consts, 2)
            dve.tensor_copy(ident16[:, :], ident[:, :]).then_inc(cast_done, 1)

        @block.tensor
        def _(pe):
            pe.wait_ge(consts, 2)
            for c in range(NJ):
                pe.wait_ge(xn_done, TI * (c + 1))
                for f in range(EC):
                    n = EC * c + f
                    if n >= 4:
                        pe.wait_ge(xnt_done, n - 3)
                    for i in range(TI):
                        last = pe.transpose(banks[n % 4][:, P * i:P * (i + 1)],
                                            xn[:, c % 2, i, P * f:P * (f + 1)], ident[:, :])
                    last.then_inc(xnt_ready, 1)


def attend(nc, wqkv, xres, ident, xnT, KS, QS, V, qscale, mask, ident16, banks, ff_weights, low_bits):
    with ExitStack() as ctx:
        sems = []

        def sem(name):
            sems.append(ctx.enter_context(nc.semaphore(name)))
            return sems[-1]

        def sb(name, shape, dt=fp32):
            return ctx.enter_context(nc.sbuf_tensor(name, shape, dt))

        PR = sb("PR", [P, NPB, GH, QB])
        wg = sb("wg", [P, EC, 3 * GE])
        qk_hi = sb("qk_hi", [P, QB], fp32r)
        qk_lo = sb("qk_lo", [P, QB], fp32r)
        acc_sb = sb("acc_sb", [P, QB])
        pm = sb("pm", [P, GH * TI, NJ])
        rowmax = sb("rowmax", [P, GH * TI])
        mneg = sb("mneg", [P, 2, GH * TI], fp32r)
        mrow = sb("mrow", [2 * GH * TI, P], fp32r)
        recip = sb("recip", [P, TI, GH, 1])
        attn = sb("attn", [P, TI, GH, D])
        low_row = sb("low_row", [1, P])
        low_part = sb("low_part", [P, 1])
        low_max = sb("low_max", [P, 1], int32)
        chunks = [xnT[:, 0, WC * slot:WC * (slot + 1)].bitcast(int32) for slot in range(2)]
        ored = xnT[:, 1, 0:WC].bitcast(int32)

        ST, MX, ACC, MISC = banks[0:NST], banks[NST:NST + NMX], banks[6], banks[7]

        wg_load = sem("wg_load")
        qk_ready = sem("qk_ready")
        hi_done = sem("hi_done")
        lo_done = sem("lo_done")
        stacked = sem("stacked")
        v_ready = sem("v_ready")
        v_done = sem("v_done")
        mx_ready = sem("mx_ready")
        mx_done = sem("mx_done")
        rowmax_done = sem("rowmax_done")
        mneg_hi = sem("mneg_hi")
        mneg_done = sem("mneg_done")
        mt_ready = sem("mt_ready")
        mrow_done = sem("mrow_done")
        max_stacked = sem("max_stacked")
        st_ready = sem("st_ready")
        exp_done = sem("exp_done")
        masked = sem("masked")
        av_done = sem("av_done")
        acc_done = sem("acc_done")
        at_ready = sem("at_ready")
        recip_done = sem("recip_done")
        attn_done = sem("attn_done")
        res_done = sem("res_done")
        first_chunk = sem("first_chunk")
        chunk_load = [sem(f"chunk_load{i}") for i in range(2)]
        or_done = sem("or_done")
        row_load = sem("row_load")

        def st_count(j, t, h):
            return GH * (TBASE[j] + t) + h + 1

        def st_bank(j, t, h):
            return ST[(st_count(j, t, h) - 1) % NST]

        def tile_count(j, t):
            return TBASE[j] + t + 1

        def weight_chunks():
            for w in ff_weights:
                r = WC // w.shape[1]
                for at in range(0, w.shape[0], P * r):
                    yield w[at:at + P * r, :].rearrange("(p r) f -> p (r f)", r=r).bitcast(int32)

        n_chunks = len(list(weight_chunks()))

        def program(g, plan):
            block = ctx_g.enter_context(nc.Block())

            @block.sync
            def _(sp):
                def load_weights():
                    if NJ - 1 in plan.preps:
                        sp.wait_ge(v_ready, plan.prep_count(NJ - 1))
                    sp.dma_start(wg[:, :, :], wqkv[bass.ds(g + 1, 1), :, :].rearrange("o p (c f) -> p (o c) f", c=EC))\
                      .then_inc(wg_load, 16)

                def stack(j, part, rows_q, rows_k):
                    for r in rows_q:
                        for h in range(GH):
                            sp.dma_start(QS[r * D:(r + 1) * D, j % NQ, h, :].bitcast(fp32),
                                         part[h * D:(h + 1) * D, :].bitcast(fp32)).then_inc(stacked, 16)
                    for r in rows_k:
                        for h in range(GH):
                            sp.dma_start(KS[r * D:(r + 1) * D, h, QB * j:QB * (j + 1)].bitcast(fp32),
                                         part[GE + h * D:GE + (h + 1) * D, :].bitcast(fp32)).then_inc(stacked, 16)

                def stack_block(J):
                    sp.wait_ge(hi_done, plan.prep_count(J))
                    stack(J % NJ, qk_hi, (0, 2), (0, 1))
                    sp.wait_ge(lo_done, plan.prep_count(J))
                    stack(J % NJ, qk_lo, (1, 3), (2, 3))

                def stack_max(J):
                    j = J % NJ
                    sp.wait_ge(mrow_done, plan.max_count(J))
                    for part in range(2):
                        sp.dma_start(QS[MROW + part:MROW + part + 1, j % NQ, :, :].bitcast(fp32),
                                     mrow[part * GH * TI:(part + 1) * GH * TI, :].bitcast(fp32)).then_inc(max_stacked, 16)

                if not plan.steps:
                    load_weights()
                    for J in plan.preps:
                        stack_block(J)
                    for J in plan.maxima:
                        stack_max(J)
                for j in plan.steps:
                    for t in range(tiles_of(j)):
                        if (j, t) == (NJ - 2, 0) and NEXT in plan.preps:
                            load_weights()
                        prepared, units = plan.stages(j, t)
                        if prepared:
                            stack_block(prepared)
                        for J, n in units:
                            if n == units_of(J) - 1:
                                stack_max(J)
                if plan is LAST:
                    sp.wait_ge(v_ready, plan.prep_count(NJ - 1))
                    for n, chunk in enumerate(weight_chunks()):
                        if n == 0:
                            sp.dma_start(ored, chunk).then_inc(first_chunk, 16)
                            continue
                        if n >= 3:
                            sp.wait_ge(or_done, n - 2)
                        sp.dma_start(chunks[n % 2], chunk).then_inc(chunk_load[n % 2], 16)
                    sp.wait_ge(or_done, n_chunks + 2)
                    sp.dma_start(low_row[:, :], low_part[:, :]).then_inc(row_load, 16)
                if NEXT in plan.preps:
                    sp.wait_ge(wg_load, 16)
                sp.wait_ge(stacked, 16 * 32 * len(plan.preps))
                sp.wait_ge(max_stacked, 32 * len(plan.maxima))

            @block.gpsimd
            def _(pool):
                for j in plan.steps:
                    for i in range(TI):
                        t = TI * j + i
                        pool.wait_ge(exp_done, st_count(j, t, GH - 1))
                        diag = PR[:, t % NPB, :, P * i:P * (i + 1)]
                        pool.affine_select(out=diag, in_=diag, compare_op=ALU.is_ge, fill=0.0, base=0,
                                           pattern=[[0, GH], [1, P]], channel_multiplier=-1).then_inc(masked, 1)

            @block.scalar
            def _(act):
                def prepare(J):
                    j, count = J % NJ, plan.prep_count(J)
                    act.wait_ge(qk_ready, count)
                    if count > 1:
                        act.wait_ge(stacked, 16 * 32 * (count - 1))
                    act.activation(qk_hi[:, :], MISC[:, :], ACT.Copy, scale=qscale[:, :]).then_inc(hi_done, 1)
                    act.wait_ge(v_ready, count)
                    act.activation(V[:, TI * j:TI * (j + 1), :, 0:D],
                                   MISC[:, 0:TI * GE].rearrange("p (i h d) -> p i h d", i=TI, h=GH),
                                   ACT.Copy).then_inc(v_done, 1)

                def copy_max(J):
                    count = plan.max_count(J)
                    act.wait_ge(mt_ready, count)
                    if count > 1:
                        act.wait_ge(max_stacked, 32 * (count - 1))
                    act.activation(mrow[:, :], MISC[0:2 * GH * TI, 0:P], ACT.Copy).then_inc(mrow_done, 1)

                def copy_acc(j):
                    act.wait_ge(av_done, tile_count(j, tiles_of(j) - 1))
                    if j >= 1:
                        act.wait_ge(at_ready, j)
                    act.activation(acc_sb[:, :], ACC[:, :], ACT.Copy).then_inc(acc_done, 1)

                if not plan.steps:
                    for J in plan.preps:
                        prepare(J)
                    for J in plan.maxima:
                        copy_max(J)
                for j in plan.steps:
                    for t in range(tiles_of(j)):
                        prepared, units = plan.stages(j, t)
                        off = max(0, P * (t - TI * j))
                        for h in range(GH):
                            act.wait_ge(st_ready, st_count(j, t, h))
                            if h == 0 and tile_count(j, t) > NPB:
                                act.wait_ge(av_done, tile_count(j, t) - NPB)
                            act.activation(PR[:, t % NPB, h, off:QB], st_bank(j, t, h)[:, off:QB], ACT.Exp)\
                               .then_inc(exp_done, 1)
                        if prepared:
                            prepare(prepared)
                        for J, n in units:
                            if n == units_of(J) - 1:
                                copy_max(J)
                    copy_acc(j)

            @block.vector
            def _(dve):
                def split(J):
                    count = plan.prep_count(J)
                    dve.wait_ge(hi_done, count)
                    if count > 1:
                        dve.wait_ge(stacked, 16 * 32 * (count - 1))
                    dve.scalar_tensor_tensor(out=qk_lo[:, :], in0=MISC[:, :], scalar=qscale[:, :],
                                             in1=qk_hi[:, :].bitcast(fp32), op0=ALU.mult, op1=ALU.subtract)\
                       .then_inc(lo_done, 1)

                def maximum(J, n):
                    h, i, c, width = max_unit(J % NJ, n)
                    v = plan.base[J] + n
                    dve.wait_ge(mx_ready, v + 1)
                    dve.reduce_max(pm[:, h * TI + i, c:c + 1], MX[v % NMX][:, 0:width], AX.X).then_inc(mx_done, 1)

                def row_maximum(J):
                    j, count = J % NJ, plan.max_count(J)
                    dve.wait_ge(mx_done, plan.base[J] + units_of(J))
                    dve.tensor_reduce(rowmax[:, :], pm[:, :, 0:j + 1], axis=AX.X, op=ALU.max).then_inc(rowmax_done, 1)
                    dve.wait_ge(rowmax_done, count)
                    if count > 1:
                        dve.wait_ge(mt_ready, count - 1)
                    dve.tensor_scalar(mneg[:, 0, :], rowmax[:, :], -1.0, None, ALU.mult).then_inc(mneg_hi, 1)
                    dve.wait_ge(mneg_hi, count)
                    dve.scalar_tensor_tensor(out=mneg[:, 1, :], in0=rowmax[:, :], scalar=-1.0,
                                             in1=mneg[:, 0, :].bitcast(fp32), op0=ALU.mult, op1=ALU.subtract)\
                       .then_inc(mneg_done, 1)

                def attention_out(j):
                    dve.wait_ge(at_ready, j + 1)
                    sums = MISC[:, :].rearrange("p (i h w) -> p i h w", i=TI, h=GH)
                    dve.reciprocal(recip[:, :, :, :], sums[:, :, :, D:D + 1]).then_inc(recip_done, 1)
                    dve.wait_ge(recip_done, j + 1)
                    dve.tensor_tensor(attn[:, :, :, :], sums[:, :, :, 0:D],
                                      recip[:, :, :, :].broadcast_to([P, TI, GH, D]), ALU.mult).then_inc(attn_done, 1)
                    dve.wait_ge(attn_done, j + 1)
                    own = xres[:, TI * j:TI * (j + 1), bass.ds(g * GE, GE)]
                    dve.tensor_tensor(own, own, attn[:, :, :, :].rearrange("p i h d -> p i (h d)"), ALU.add)\
                       .then_inc(res_done, 1)

                def test_weights():
                    dve.wait_ge(first_chunk, 16)
                    for n in range(1, n_chunks):
                        dve.wait_ge(chunk_load[n % 2], 16 * ((n + 1) // 2))
                        if n >= 2:
                            dve.wait_ge(or_done, n - 1)
                        dve.tensor_tensor(ored, ored, chunks[n % 2], ALU.bitwise_or).then_inc(or_done, 1)
                    dve.wait_ge(or_done, n_chunks - 1)
                    dve.tensor_scalar(ored, ored, 2 ** LOW_BITS - 1, None, ALU.bitwise_and).then_inc(or_done, 1)
                    dve.wait_ge(or_done, n_chunks)
                    dve.tensor_reduce(low_max[:, :], ored, axis=AX.X, op=ALU.max).then_inc(or_done, 1)
                    dve.wait_ge(or_done, n_chunks + 1)
                    dve.tensor_copy(low_part[:, :], low_max[:, :]).then_inc(or_done, 1)
                    dve.wait_ge(row_load, 16)
                    dve.tensor_reduce(low_bits[:, :], low_row[:, :], axis=AX.X, op=ALU.max).then_inc(or_done, 1)
                    dve.wait_ge(or_done, n_chunks + 3)

                if not plan.steps:
                    for J in plan.preps:
                        split(J)
                    for J, n in plan.rest:
                        maximum(J, n)
                    for J in plan.maxima:
                        row_maximum(J)
                for j in plan.steps:
                    for t in range(tiles_of(j)):
                        prepared, units = plan.stages(j, t)
                        for J, n in units:
                            maximum(J, n)
                            if n == units_of(J) - 1:
                                row_maximum(J)
                        if t == 0 and j > 0:
                            attention_out(j - 1)
                        if prepared:
                            split(prepared)
                if plan is LAST:
                    test_weights()
                if plan.steps:
                    attention_out(NJ - 1)

            @block.tensor
            def _(pe):
                def misc_free(kind, j):
                    at = plan.misc.index((kind, j))
                    if at == 0:
                        return
                    kind, j = plan.misc[at - 1]
                    if kind == "qk":
                        pe.wait_ge(lo_done, plan.prep_count(j))
                    if kind == "v":
                        pe.wait_ge(v_done, plan.prep_count(j))
                    if kind == "max":
                        pe.wait_ge(mrow_done, plan.max_count(j))
                    if kind == "acc":
                        pe.wait_ge(attn_done, j + 1)

                def project(J):
                    j = J % NJ
                    if J == NEXT:
                        pe.wait_ge(wg_load, 16)
                    misc_free("qk", J)
                    for c in range(EC):
                        last = pe.matmul(MISC[:, :], wg[:, c, 0:2 * GE], xnT[:, c, QB * j:QB * (j + 1)],
                                         start=(c == 0), stop=(c == EC - 1))
                    last.then_inc(qk_ready, 1)
                    misc_free("v", J)
                    for i in range(TI):
                        at = QB * j + P * i
                        for c in range(EC):
                            last = pe.matmul(MISC[:, GE * i:GE * (i + 1)], xnT[:, c, at:at + P],
                                             wg[:, c, 2 * GE:3 * GE], start=(c == 0), stop=(c == EC - 1))
                    last.then_inc(v_ready, 1)

                def maximum(J, n):
                    j = J % NJ
                    h, i, c, width = max_unit(j, n)
                    v = plan.base[J] + n
                    if n == 0 and J in plan.preps:
                        pe.wait_ge(stacked, 16 * 32 * plan.prep_count(J))
                    if v >= NMX:
                        pe.wait_ge(mx_done, v - NMX + 1)
                    diagonal = c == j
                    last = pe.matmul(MX[v % NMX][:, 0:width], QS[0:MROW, j % NQ, h, P * i:P * (i + 1)],
                                     KS[0:MROW, h, QB * c:QB * c + width], start=True, stop=not diagonal)
                    if diagonal:
                        last = pe.matmul(MX[v % NMX][:, width - P:width], ident16[:, :], mask[:, :],
                                         start=False, stop=True)
                    last.then_inc(mx_ready, 1)

                def transpose_max(J):
                    misc_free("max", J)
                    pe.wait_ge(mneg_done, plan.max_count(J))
                    pe.transpose(MISC[0:2 * GH * TI, 0:P], mneg[:, :, :].rearrange("p a n -> p (a n)").bitcast(fp32),
                                 ident[:, :]).then_inc(mt_ready, 1)

                def score(j, t, h):
                    off = max(0, P * (t - TI * j))
                    if t == 0 and h == 0 and j in plan.maxima:
                        pe.wait_ge(max_stacked, 32 * plan.max_count(j))
                    if st_count(j, t, h) > NST:
                        pe.wait_ge(exp_done, st_count(j, t, h) - NST)
                    pe.matmul(st_bank(j, t, h)[:, off:QB], KS[:, h, P * t:P * (t + 1)], QS[:, j % NQ, h, off:QB],
                              start=True, stop=True).then_inc(st_ready, 1)

                def product(j, t):
                    off = max(0, P * (t - TI * j))
                    if t == 0:
                        if j >= 1:
                            pe.wait_ge(acc_done, j)
                        if j in plan.preps:
                            pe.wait_ge(v_done, plan.prep_count(j))
                    if t >= TI * j:
                        pe.wait_ge(masked, t + 1)
                    pe.wait_ge(exp_done, st_count(j, t, GH - 1))
                    for h in range(GH):
                        last = pe.matmul(ACC[VW * h:VW * (h + 1), off:QB], V[:, t, h, :], PR[:, t % NPB, h, off:QB],
                                         start=(t == 0), stop=(t == tiles_of(j) - 1))
                    last.then_inc(av_done, 1)

                def transpose_acc(j):
                    misc_free("acc", j)
                    pe.wait_ge(acc_done, j + 1)
                    for i in range(TI):
                        last = pe.transpose(MISC[:, P * i:P * (i + 1)], acc_sb[:, P * i:P * (i + 1)], ident[:, :])
                    last.then_inc(at_ready, 1)

                if not plan.steps:
                    for J in plan.preps:
                        project(J)
                    for J, n in plan.rest:
                        maximum(J, n)
                    for J in plan.maxima:
                        transpose_max(J)
                for j in plan.steps:
                    for t in range(tiles_of(j)):
                        prepared, units = plan.stages(j, t)
                        for h in range(GH):
                            score(j, t, h)
                            for J, n in units[len(units) * h // GH:len(units) * (h + 1) // GH]:
                                maximum(J, n)
                            if h == AV_AFTER and t > 0:
                                product(j, t - 1)
                        if t == 0 and j > 0:
                            transpose_acc(j - 1)
                        if prepared:
                            project(prepared)
                        for J, n in units:
                            if n == units_of(J) - 1:
                                transpose_max(J)
                    product(j, tiles_of(j) - 1)
                if plan.steps:
                    transpose_acc(NJ - 1)

        with ExitStack() as ctx_g:
            program(-1, START)
        clear(nc, sems)
        with nc.Fori(0, G - 1) as g:
            with ExitStack() as ctx_g:
                program(g, GROUP)
            clear(nc, sems)
        with ExitStack() as ctx_g:
            program(G - 1, LAST)


def feed_forward_exact(nc, w1, s1, w2, s2, h1w, h1s, h2w, h2s, w3, s3, out, xres, ident, eps, banks):
    with ExitStack() as ctx:
        sems = []

        def sem(name, kept=False):
            s = ctx.enter_context(nc.semaphore("e_" + name))
            if not kept:
                sems.append(s)
            return s

        def sb(name, shape, dt=fp32):
            return ctx.enter_context(nc.sbuf_tensor("e_" + name, shape, dt))

        NB = 4
        NR, NTMP = 6, 4
        RING, TB = banks[0:NR], banks[6:8]
        UNITS = 3 * FC
        NS = 2 * TI
        NY = 3 * TI

        w1_sb = sb("w1_sb", [P, EC, FF], fp32r)
        w2_sb = sb("w2_sb", [P, EC, FF], fp32r)
        h1_sb = sb("h1_sb", [P, FC, FF], fp32r)
        h2_sb = sb("h2_sb", [P, FC, FF], fp32r)
        w3_sb = sb("w3_sb", [P, FC, E], fp32r)
        s_sb = sb("s_sb", [P, 4, FC])
        s3_sb = sb("s3_sb", [P, E])
        x1T = sb("x1T", [P, 2, EC, QB], fp32r)
        hid = sb("hid", [P, 2, 2, FC, QB], fp32r)
        tmp = sb("tmp", [P, NTMP, QB])
        y = sb("y", [P, TI, E])
        stats = sb("stats", [P, TI, 6])
        mv = sb("mv", [P, TI, 2])
        std = sb("std", [P, TI, 1])
        rstd = sb("rstd", [P, TI, 1])
        ystats = sb("y_stats", [P, TI, 6])
        ymv = sb("y_mv", [P, TI, 2])
        ystd = sb("y_std_sb", [P, TI, 1])
        yrstd = sb("y_rstd_sb", [P, TI, 1])

        w_load = [sem(f"w_load{i}", kept=True) for i in range(5)]
        s_load = sem("s_load", kept=True)
        x1_stat = sem("x1_stat")
        x1_std = sem("x1_std")
        x1_rstd = sem("x1_rstd")
        x1_done = sem("x1_done")
        x1_kept = sem("x1_kept")
        x1t_ready = sem("x1t_ready")
        x1t_hi = sem("x1t_hi")
        x1t_lo = sem("x1t_lo")
        glu_ready = sem("glu_ready")
        silu_done = sem("silu_done")
        glu_done = sem("glu_done")
        hid_ready = sem("hid_ready")
        gelu_done = sem("gelu_done")
        hi_done = sem("hi_done")
        parts_done = sem("parts_done")
        y_ready = sem("y_ready")
        y_done = sem("y_done")
        y_stat = sem("y_stat")
        y_std = sem("y_std")
        y_rstd = sem("y_rstd")
        o_done = sem("o_done")
        stored = sem("stored")

        def unit(T, n):
            return UNITS * T + n

        def program(b):
            block = ctx_b.enter_context(nc.Block())

            @block.sync
            def _(sp):
                for T in range(NB):
                    sp.wait_ge(o_done, T + 1)
                    sp.dma_start(out_v[bass.ds(NB * b + T, 1), :, :, :].rearrange("o p t e -> p (o t) e"),
                                 y[:, :, :]).then_inc(stored, 16)
                sp.wait_ge(stored, 16 * NB)

            @block.gpsimd
            def _(pool):
                pool.wait_ge(stored, 16 * NB)

            @block.scalar
            def _(act):
                def std_x1(T):
                    act.wait_ge(x1_stat, NS * (T + 1))
                    act.activation(std[:, :, :], mv[:, :, 1:2], ACT.Sqrt, bias=eps[:, :]).then_inc(x1_std, 1)

                def std_y(T):
                    act.wait_ge(y_stat, NY * (T + 1))
                    act.activation(ystd[:, :, :], ymv[:, :, 1:2], ACT.Sqrt, bias=eps[:, :]).then_inc(y_std, 1)

                def copy_x1T(T):
                    for f in range(EC):
                        act.wait_ge(x1t_ready, EC * T + f + 1)
                        act.activation(x1T[:, 0, f, :], TB[f][:, :], ACT.Copy).then_inc(x1t_hi, 1)

                def gated_hi(T, o):
                    act.wait_ge(glu_done, FC * T + o + 1)
                    act.activation(hid[:, T % 2, 0, o, :], tmp[:, unit(T, o) % NTMP, :], ACT.Copy).then_inc(hi_done, 1)

                def tmp_free(u):
                    if u >= NTMP:
                        act.wait_ge(parts_done, u - NTMP + 1)

                std_x1(0)
                copy_x1T(0)
                for T in range(NB):
                    for o in range(FC):
                        act.wait_ge(glu_ready, FC * T + o + 1)
                        tmp_free(unit(T, o))
                        act.activation(tmp[:, unit(T, o) % NTMP, :], RING[2 * (o % 3)][:, :], ACT.Silu,
                                       scale=s_sb[:, 0, o:o + 1]).then_inc(silu_done, 1)
                        if o > 0:
                            gated_hi(T, o - 1)
                    gated_hi(T, FC - 1)
                    for n in range(2 * FC):
                        u = unit(T, FC + n)
                        act.wait_ge(hid_ready, 2 * FC * T + n + 1)
                        tmp_free(u)
                        act.activation(tmp[:, u % NTMP, :], RING[(4 + n) % NR][:, :], ACT.Gelu,
                                       scale=s_sb[:, 2 + n // FC, n % FC:n % FC + 1]).then_inc(gelu_done, 1)
                        if n == 4:
                            if T > 0:
                                std_y(T - 1)
                            if T < NB - 1:
                                std_x1(T + 1)
                    if T < NB - 1:
                        copy_x1T(T + 1)
                std_y(NB - 1)

            @block.vector
            def _(dve):
                def tokens(T):
                    return [xres[:, bass.ds(TI * NB * b + TI * T + i, 1), :].rearrange("p o e -> p (o e)")
                            for i in range(TI)]

                def x1_statistics(T):
                    for i in range(TI):
                        dve.bn_stats(stats[:, i, :], tokens(T)[i]).then_inc(x1_stat, 1)
                    dve.wait_ge(x1_stat, NS * T + TI)
                    for i in range(TI):
                        dve.bn_aggr(mv[:, i, :], stats[:, i, :]).then_inc(x1_stat, 1)

                def x1_normalise(T):
                    dve.wait_ge(x1_std, T + 1)
                    if T >= 2:
                        dve.wait_ge(stored, 16 * (T - 1))
                    dve.reciprocal(rstd[:, :, :], std[:, :, :]).then_inc(x1_rstd, 1)
                    dve.wait_ge(x1_rstd, T + 1)
                    for i in range(TI):
                        dve.tensor_scalar(y[:, i, :], tokens(T)[i], mv[:, i, 0:1], rstd[:, i, :],
                                          ALU.subtract, ALU.mult).then_inc(x1_done, 1)
                    for i in range(TI):
                        own = tokens(T)[i]
                        dve.tensor_scalar(own, own, mv[:, i, 0:1], rstd[:, i, :],
                                          ALU.subtract, ALU.mult).then_inc(x1_kept, 1)

                def x1T_low(T):
                    for f in range(EC):
                        dve.wait_ge(x1t_hi, EC * T + f + 1)
                        dve.tensor_tensor(x1T[:, 1, f, :], TB[f][:, :], x1T[:, 0, f, :].bitcast(fp32), ALU.subtract)\
                           .then_inc(x1t_lo, 1)

                def low_part(u, buffer, c):
                    dve.wait_ge(hi_done, u + 1)
                    dve.tensor_tensor(hid[:, buffer, 1, c, :], tmp[:, u % NTMP, :],
                                      hid[:, buffer, 0, c, :].bitcast(fp32), ALU.subtract).then_inc(parts_done, 1)

                def y_read(T):
                    if T > 0:
                        dve.wait_ge(stored, 16 * T)
                    dve.wait_ge(y_ready, T + 1)
                    for i in range(TI):
                        dve.tensor_tensor(y[:, i, :], RING[2 + i][:, 0:E], s3_sb[:, :], ALU.mult).then_inc(y_done, 1)

                def y_statistics(T):
                    for i in range(TI):
                        dve.wait_ge(y_done, TI * T + i + 1)
                        dve.wait_ge(x1_kept, TI * T + i + 1)
                        dve.tensor_tensor(y[:, i, :], y[:, i, :], tokens(T)[i], ALU.add).then_inc(y_stat, 1)
                    for i in range(TI):
                        dve.wait_ge(y_stat, NY * T + i + 1)
                        dve.bn_stats(ystats[:, i, :], y[:, i, :]).then_inc(y_stat, 1)
                    dve.wait_ge(y_stat, NY * T + 2 * TI)
                    for i in range(TI):
                        dve.bn_aggr(ymv[:, i, :], ystats[:, i, :]).then_inc(y_stat, 1)

                def y_normalise(T):
                    dve.wait_ge(y_std, T + 1)
                    dve.reciprocal(yrstd[:, :, :], ystd[:, :, :]).then_inc(y_rstd, 1)
                    dve.wait_ge(y_rstd, T + 1)
                    for i in range(TI):
                        last = dve.tensor_scalar(y[:, i, :], y[:, i, :], ymv[:, i, 0:1], yrstd[:, i, :],
                                                 ALU.subtract, ALU.mult)
                    last.then_inc(o_done, 1)

                x1_statistics(0)
                x1_normalise(0)
                x1T_low(0)
                for T in range(NB):
                    if T > 0:
                        y_read(T - 1)
                    for o in range(FC):
                        u = unit(T, o)
                        dve.wait_ge(silu_done, FC * T + o + 1)
                        dve.scalar_tensor_tensor(out=tmp[:, u % NTMP, :], in0=RING[2 * (o % 3) + 1][:, :],
                                                 scalar=s_sb[:, 1, o:o + 1], in1=tmp[:, u % NTMP, :],
                                                 op0=ALU.mult, op1=ALU.mult).then_inc(glu_done, 1)
                        if o > 0:
                            low_part(u - 1, T % 2, o - 1)
                    low_part(unit(T, FC - 1), T % 2, FC - 1)
                    if T > 0:
                        y_statistics(T - 1)
                    for n in range(2 * FC):
                        u = unit(T, FC + n)
                        buffer = (T + 1 + n // FC) % 2
                        dve.wait_ge(gelu_done, 2 * FC * T + n + 1)
                        dve.tensor_copy(hid[:, buffer, 0, n % FC, :], tmp[:, u % NTMP, :]).then_inc(hi_done, 1)
                        low_part(u, buffer, n % FC)
                        if n == 2 and T < NB - 1:
                            x1_statistics(T + 1)
                        if n == 5 and T > 0:
                            y_normalise(T - 1)
                        if n == 9 and T < NB - 1:
                            x1_normalise(T + 1)
                    if T < NB - 1:
                        x1T_low(T + 1)
                y_read(NB - 1)
                y_statistics(NB - 1)
                y_normalise(NB - 1)

            @block.tensor
            def _(pe):
                def transpose_x1(T):
                    pe.wait_ge(x1_done, TI * (T + 1))
                    for f in range(EC):
                        for i in range(TI):
                            last = pe.transpose(TB[f][:, P * i:P * (i + 1)], y[:, i, P * f:P * (f + 1)], ident[:, :])
                        last.then_inc(x1t_ready, 1)

                transpose_x1(0)
                for T in range(NB):
                    for o in range(FC):
                        if T > 0 and o in (1, 2):
                            pe.wait_ge(y_done, TI * (T - 1) + 2 * o)
                        if o >= 3:
                            pe.wait_ge(glu_done, FC * T + o - 2)
                        for w, at in ((w1_sb, 0), (w2_sb, 1)):
                            for c in range(EC):
                                if o == 0 and at == 0:
                                    pe.wait_ge(x1t_lo, EC * T + c + 1)
                                for part in range(2):
                                    last = pe.matmul(RING[2 * (o % 3) + at][:, :], w[:, c, P * o:P * (o + 1)],
                                                     x1T[:, part, c, :], start=(c == 0 and part == 0),
                                                     stop=(c == EC - 1 and part == 1))
                        last.then_inc(glu_ready, 1)
                    for n in range(2 * FC):
                        layer, o = divmod(n, FC)
                        w = (h1_sb, h2_sb)[layer]
                        if n == 0:
                            pe.wait_ge(glu_done, FC * T + NR)
                        if n >= NR:
                            pe.wait_ge(gelu_done, 2 * FC * T + n - NR + 1)
                        for c in range(FC):
                            if o == 0:
                                pe.wait_ge(parts_done, unit(T, FC * layer) + c + 1)
                            for part in range(2):
                                last = pe.matmul(RING[(4 + n) % NR][:, :], w[:, c, P * o:P * (o + 1)],
                                                 hid[:, (T + layer) % 2, part, c, :], start=(c == 0 and part == 0),
                                                 stop=(c == FC - 1 and part == 1))
                        last.then_inc(hid_ready, 1)
                    if T < NB - 1:
                        transpose_x1(T + 1)
                    pe.wait_ge(gelu_done, 2 * FC * T + FC + TI + 2)
                    for c in range(FC):
                        pe.wait_ge(parts_done, unit(T, 2 * FC) + c + 1)
                        for i in range(TI):
                            for part in range(2):
                                last = pe.matmul(RING[2 + i][:, 0:E], hid[:, T % 2, part, c, P * i:P * (i + 1)],
                                                 w3_sb[:, c, :], start=(c == 0 and part == 0),
                                                 stop=(c == FC - 1 and part == 1))
                    last.then_inc(y_ready, 1)

        with ExitStack() as ctx_l:
            block = ctx_l.enter_context(nc.Block())

            @block.sync
            def _(sp):
                for v, s in enumerate((s1, s2, h1s, h2s)):
                    sp.dma_start(s_sb[:, v, :], s).then_inc(s_load, 16)
                sp.dma_start(s3_sb[:, :], s3.rearrange("(o e) -> o e", o=1).broadcast_to([P, E])).then_inc(s_load, 16)
                sp.wait_ge(s_load, 16 * 5)

            @block.gpsimd
            def _(pool):
                for n, (dst, src) in enumerate(((w1_sb, w1), (w2_sb, w2), (h1_sb, h1w), (h2_sb, h2w), (w3_sb, w3))):
                    pool.dma_start(dst[:, :, :], src.rearrange("(c p) f -> p c f", p=P)).then_inc(w_load[n], 16)
                for n in range(5):
                    pool.wait_ge(w_load[n], 16)

        out_v = out.rearrange("o (b t p) e -> b p (o t) e", p=P, t=TI)
        with nc.Fori(0, NJ // NB) as b:
            with ExitStack() as ctx_b:
                program(b)
            clear(nc, sems)


def feed_forward(nc, w1, s1, w2, s2, h1w, h1s, h2w, h2s, w3, s3, out, xres, ident, eps, banks):
    with ExitStack() as ctx:
        sems = []

        def sem(name, kept=False):
            s = ctx.enter_context(nc.semaphore(name))
            if not kept:
                sems.append(s)
            return s

        def sb(name, shape, dt=fp32):
            return ctx.enter_context(nc.sbuf_tensor(name, shape, dt))

        w1_sb = sb("w1_sb", [P, EC, FF])
        w2_sb = sb("w2_sb", [P, EC, FF])
        h1_sb = sb("h1_sb", [P, FC, FF])
        h2_sb = sb("h2_sb", [P, FC, FF])
        w3_sb = sb("w3_sb", [P, FC, E])
        s_sb = sb("s_sb", [P, 4, FC])
        s3_sb = sb("s3_sb", [P, E])
        x1 = sb("x1", [P, 2, TI, E])
        x1T = sb("x1T", [P, 2, EC, QB])
        hid = sb("hid", [P, 3, FC, QB])
        gate = sb("gate", [P, 2, QB])
        stats = sb("ff_stats", [P, TI, 6])
        mv = sb("ff_mv", [P, TI, 2])
        std = sb("ff_std", [P, TI, 1])
        rstd = sb("ff_rstd", [P, TI, 1])
        ystats = sb("y_stats", [P, TI, 6])
        ymv = sb("y_mv", [P, TI, 2])
        ystd = sb("y_std_sb", [P, TI, 1])
        yrstd = sb("y_rstd_sb", [P, TI, 1])
        y = sb("y", [P, 2, TI, E])
        o_sb = sb("o_sb", [P, 2, TI, E])

        NR = 6
        RING, TB = banks[0:NR], banks[6:8]
        NS, NY = 2 * TI, 3 * TI

        w_load = [sem(f"w_load{i}", kept=True) for i in range(5)]
        s_load = sem("s_load", kept=True)
        x1_stat = sem("x1_stat")
        x1_std = sem("x1_std")
        x1_rstd = sem("x1_rstd")
        y_std = sem("y_std")
        y_rstd = sem("y_rstd")
        x1_done = sem("x1_done")
        x1t_ready = sem("x1t_ready")
        x1t_done = sem("x1t_done")
        glu_ready = sem("glu_ready")
        silu_done = sem("silu_done")
        glu_done = sem("glu_done")
        hid_ready = sem("hid_ready")
        gelu_done = sem("gelu_done")
        y_ready = sem("y_ready")
        y_done = sem("y_done")
        y_stat = sem("y_stat")
        o_done = sem("o_done")
        stored = sem("stored")

        def program(b):
            block = ctx_b.enter_context(nc.Block())

            @block.sync
            def _(sp):
                for T in range(2):
                    sp.wait_ge(o_done, T + 1)
                    sp.dma_start(out_v[bass.ds(2 * b + T, 1), :, :, :].rearrange("o p t e -> p (o t) e"),
                                 o_sb[:, T, :, :]).then_inc(stored, 16)
                sp.wait_ge(stored, 32)

            @block.scalar
            def _(act):
                def copy_x1T(T):
                    for f in range(EC):
                        act.wait_ge(x1t_ready, EC * T + f + 1)
                        act.activation(x1T[:, T, f, :], TB[f][:, :], ACT.Copy).then_inc(x1t_done, 1)

                def std_x1(T):
                    act.wait_ge(x1_stat, NS * (T + 1))
                    act.activation(std[:, :, :], mv[:, :, 1:2], ACT.Sqrt, bias=eps[:, :]).then_inc(x1_std, 1)

                def std_y(T):
                    act.wait_ge(y_stat, NY * (T + 1))
                    act.activation(ystd[:, :, :], ymv[:, :, 1:2], ACT.Sqrt, bias=eps[:, :]).then_inc(y_std, 1)

                std_x1(0)
                copy_x1T(0)
                for T in range(2):
                    for o in range(FC):
                        n = FC * T + o
                        act.wait_ge(glu_ready, n + 1)
                        if n >= 2:
                            act.wait_ge(glu_done, n - 1)
                        act.activation(gate[:, n % 2, :], RING[2 * (o % 3)][:, :], ACT.Silu,
                                       scale=s_sb[:, 0, o:o + 1]).then_inc(silu_done, 1)
                    if T == 0:
                        std_x1(1)
                    else:
                        std_y(0)
                    for layer in range(2):
                        for o in range(FC):
                            n = FC * layer + o
                            act.wait_ge(hid_ready, 2 * FC * T + n + 1)
                            if T == 1 and layer == 1 and o == 0:
                                act.wait_ge(y_ready, TI)
                            act.activation(hid[:, layer + 1, o, :], RING[(4 + n) % NR][:, :], ACT.Gelu,
                                           scale=s_sb[:, 2 + layer, o:o + 1]).then_inc(gelu_done, 1)
                    if T == 0:
                        copy_x1T(1)
                    else:
                        std_y(1)

            @block.vector
            def _(dve):
                def layernorm_x1(T):
                    tok = [xres[:, bass.ds(2 * TI * b + TI * T + i, 1), :].rearrange("p o e -> p (o e)")
                           for i in range(TI)]
                    for i in range(TI):
                        dve.bn_stats(stats[:, i, :], tok[i]).then_inc(x1_stat, 1)
                    dve.wait_ge(x1_stat, NS * T + TI)
                    for i in range(TI):
                        dve.bn_aggr(mv[:, i, :], stats[:, i, :]).then_inc(x1_stat, 1)
                    dve.wait_ge(x1_std, T + 1)
                    dve.reciprocal(rstd[:, :, :], std[:, :, :]).then_inc(x1_rstd, 1)
                    dve.wait_ge(x1_rstd, T + 1)
                    for i in range(TI):
                        dve.tensor_scalar(x1[:, T, i, :], tok[i], mv[:, i, 0:1], rstd[:, i, :],
                                          ALU.subtract, ALU.mult).then_inc(x1_done, 1)

                def gated(T):
                    for o in range(FC):
                        n = FC * T + o
                        dve.wait_ge(silu_done, n + 1)
                        dve.scalar_tensor_tensor(out=hid[:, 0, o, :], in0=RING[2 * (o % 3) + 1][:, :],
                                                 scalar=s_sb[:, 1, o:o + 1], in1=gate[:, n % 2, :],
                                                 op0=ALU.mult, op1=ALU.mult).then_inc(glu_done, 1)

                def residual(T):
                    for i in range(TI):
                        dve.wait_ge(y_ready, TI * T + i + 1)
                        dve.tensor_tensor(y[:, T, i, :], RING[2 + i][:, 0:E], s3_sb[:, :], ALU.mult).then_inc(y_done, 1)
                    for i in range(TI):
                        dve.wait_ge(y_done, TI * T + i + 1)
                        dve.tensor_tensor(y[:, T, i, :], y[:, T, i, :], x1[:, T, i, :], ALU.add).then_inc(y_stat, 1)
                    for i in range(TI):
                        dve.wait_ge(y_stat, NY * T + i + 1)
                        dve.bn_stats(ystats[:, i, :], y[:, T, i, :]).then_inc(y_stat, 1)
                    dve.wait_ge(y_stat, NY * T + 2 * TI)
                    for i in range(TI):
                        dve.bn_aggr(ymv[:, i, :], ystats[:, i, :]).then_inc(y_stat, 1)

                def output(T):
                    dve.wait_ge(y_std, T + 1)
                    dve.reciprocal(yrstd[:, :, :], ystd[:, :, :]).then_inc(y_rstd, 1)
                    dve.wait_ge(y_rstd, T + 1)
                    for i in range(TI):
                        last = dve.tensor_scalar(o_sb[:, T, i, :], y[:, T, i, :], ymv[:, i, 0:1], yrstd[:, i, :],
                                                 ALU.subtract, ALU.mult)
                    last.then_inc(o_done, 1)

                layernorm_x1(0)
                gated(0)
                layernorm_x1(1)
                residual(0)
                gated(1)
                output(0)
                residual(1)
                output(1)

            @block.tensor
            def _(pe):
                def transpose_x1(T):
                    pe.wait_ge(x1_done, TI * (T + 1))
                    for f in range(EC):
                        for i in range(TI):
                            last = pe.transpose(TB[f][:, P * i:P * (i + 1)], x1[:, T, i, P * f:P * (f + 1)],
                                                ident[:, :])
                        last.then_inc(x1t_ready, 1)

                transpose_x1(0)
                for T in range(2):
                    pe.wait_ge(x1t_done, EC * (T + 1))
                    for o in range(FC):
                        if T == 1 and o in (1, 2):
                            pe.wait_ge(y_done, 2 * o)
                        if o >= 3:
                            pe.wait_ge(glu_done, FC * T + o - 2)
                        for w, at in ((w1_sb, 0), (w2_sb, 1)):
                            for c in range(EC):
                                last = pe.matmul(RING[2 * (o % 3) + at][:, :], w[:, c, P * o:P * (o + 1)],
                                                 x1T[:, T, c, :], start=(c == 0), stop=(c == EC - 1))
                        last.then_inc(glu_ready, 1)
                    for layer in range(2):
                        w = (h1_sb, h2_sb)[layer]
                        for o in range(FC):
                            n = FC * layer + o
                            if n >= NR:
                                pe.wait_ge(gelu_done, 2 * FC * T + n - NR + 1)
                            for c in range(FC):
                                if layer == 0 and o == 0:
                                    pe.wait_ge(glu_done, FC * T + max(c, NR - 1) + 1)
                                if layer == 1 and o == 0:
                                    pe.wait_ge(gelu_done, 2 * FC * T + c + 1)
                                last = pe.matmul(RING[(4 + n) % NR][:, :], w[:, c, P * o:P * (o + 1)],
                                                 hid[:, layer, c, :], start=(c == 0), stop=(c == FC - 1))
                            last.then_inc(hid_ready, 1)
                    if T == 0:
                        transpose_x1(1)
                    for i in range(TI):
                        for c in range(FC):
                            if i == 0:
                                pe.wait_ge(gelu_done, 2 * FC * T + FC + max(c, TI + 1) + 1)
                            last = pe.matmul(RING[2 + i][:, 0:E], hid[:, 2, c, P * i:P * (i + 1)], w3_sb[:, c, :],
                                             start=(c == 0), stop=(c == FC - 1))
                        last.then_inc(y_ready, 1)

        with ExitStack() as ctx_l:
            block = ctx_l.enter_context(nc.Block())

            @block.sync
            def _(sp):
                for v, s in enumerate((s1, s2, h1s, h2s)):
                    sp.dma_start(s_sb[:, v, :], s).then_inc(s_load, 16)
                sp.dma_start(s3_sb[:, :], s3.rearrange("(o e) -> o e", o=1).broadcast_to([P, E])).then_inc(s_load, 16)
                for n, (dst, src) in enumerate(((w1_sb, w1), (w2_sb, w2), (h1_sb, h1w), (h2_sb, h2w), (w3_sb, w3))):
                    sp.dma_start(dst[:, :, :], src.rearrange("(c p) f -> p c f", p=P)).then_inc(w_load[n], 16)
                sp.wait_ge(s_load, 16 * 5)
                for n in range(5):
                    sp.wait_ge(w_load[n], 16)

        out_v = out.rearrange("o (b t p) e -> b p (o t) e", p=P, t=TI)
        with nc.Fori(0, NJ // 2) as b:
            with ExitStack() as ctx_b:
                program(b)
            clear(nc, sems)


_OUTS = [((1, S, E), "float32")]


def kernel(**inputs):
    import numpy as _np
    import concourse.bacc as _bacc
    from concourse import mybir as _mybir
    from concourse.bass_utils import run_bass_kernel_spmd as _run

    w = _np.asarray(inputs["L0_attn_w_qkv"]).reshape(3, G, GE, EC, P)
    wqkv = _np.ascontiguousarray(w.transpose(1, 4, 3, 0, 2).reshape(G, P, EC * 3 * GE))

    def by_chunk(v):
        return _np.asarray(v).reshape(-1, P).T

    laid = {
        "x": inputs["L0_attn_x"], "gamma": by_chunk(inputs["L0_attn_gamma"]),
        "beta": by_chunk(inputs["L0_attn_beta"]), "wqkv": wqkv,
        "w1": _np.asarray(inputs["L0_ffn_w1_w"]).T, "s1": by_chunk(inputs["L0_ffn_w1_s"]),
        "w2": _np.asarray(inputs["L0_ffn_w2_w"]).T, "s2": by_chunk(inputs["L0_ffn_w2_s"]),
        "h1": _np.asarray(inputs["L0_ffn_h1_w"]).T, "h1s": by_chunk(inputs["L0_ffn_h1_s"]),
        "h2": _np.asarray(inputs["L0_ffn_h2_w"]).T, "h2s": by_chunk(inputs["L0_ffn_h2_s"]),
        "w3": _np.asarray(inputs["L0_ffn_w3_w"]).T, "s3": inputs["L0_ffn_w3_s"],
    }
    nc = _bacc.Bacc("TRN2", target_bir_lowering=False, num_devices=1)
    arrays, args = {}, []
    for name, a in laid.items():
        a = _np.ascontiguousarray(a)
        arrays[f"in_{name}_dram"] = a
        args.append(nc.dram_tensor(f"in_{name}_dram", a.shape, _mybir.dt.from_np(a.dtype), kind="ExternalInput").ap())
    for i, (shape, dtype) in enumerate(_OUTS):
        args.append(nc.dram_tensor(f"out_{i}_dram", shape, _mybir.dt.from_np(_np.dtype(dtype)), kind="ExternalOutput").ap())
    block_kernel(nc, *args)
    r = _run(nc, [arrays], core_ids=[0])
    return r.results[0]["out_0_dram"]
```

```python
import concourse.bass as bass
from concourse import mybir
from contextlib import ExitStack

fp32 = mybir.dt.float32
fp32r = mybir.dt.float32r
bf16 = mybir.dt.bfloat16
int32 = mybir.dt.int32
ALU = mybir.AluOpType
ACT = mybir.ActivationFunctionType
AX = mybir.AxisListType

S, E, H, FF = 4096, 256, 16, 1024
D = E // H
P = 128
EC, FC = E // P, FF // P
QB = 512
NJ = S // QB
TI = QB // P
G, GH = 4, 4
GE = GH * D
LOW_BITS = 12
WC = 2048
EPS = 1e-5
MASK = -1e30
VW = 32
ROWS = 4 * D
MROW = P - 2
NORM_RING = 3
NRING, NPB = 7, 2
AV_AFTER = 2
NQ = 4


def tiles_of(j):
    return TI * (j + 1)


TBASE = [sum(tiles_of(i) for i in range(j)) for j in range(NJ + 1)]


def max_unit(j, n):
    h, rest = divmod(n, TI * (j + 1))
    i, c = divmod(rest, j + 1)
    return h, i, c, QB if c < j else P * (i + 1)


NEXT = NJ


def units_of(J):
    return GH * TI * (J % NJ + 1)


def with_head(units, h):
    return units[len(units) * h // GH:len(units) * (h + 1) // GH]


class Plan:

    def __init__(self, steps, preps, maxima):
        self.steps, self.preps, self.maxima = steps, preps, maxima
        self.base = {J: sum(units_of(i) for i in maxima if i < J) for J in maxima}
        ahead = [(J, n) for J in maxima for n in range(units_of(J))]
        self.work, at = {}, 0
        for j in steps:
            for t in range(tiles_of(j)):
                self.work[j, t] = ([], [])
        for j in steps:
            T = tiles_of(j)
            goal = min(len(ahead), sum(1 for J, _ in ahead if J <= j + 1) + LEAD[j])
            first = NEXT_MAX_AT if j == NJ - 1 else 0
            begin, stop = at, T - STOP[j]
            for t in range(T):
                upto = begin + (goal - begin) * max(0, min(t + 1, stop) - first) // (stop - first)
                self.work[j, t][0].extend(ahead[at:upto])
                for J, n in ahead[at:upto]:
                    if n == units_of(J) - 1:
                        self.work[j, t][1].append(("max", J))
                if t == ACC_AT and j > 0:
                    self.work[j, t][1].append(("acc", j - 1))
                for J, where in preps.items():
                    if where == (j, t):
                        self.work[j, t][1].append(("qk", J))
                        self.work[j, t + 1][1].append(("v", J))
                at = upto
        order = []
        if not steps:
            for kind, J in START_ORDER:
                if kind == "max":
                    order += [("unit", J, n) for n in range(units_of(J))]
                if kind in ("qk", "v", "max"):
                    order.append((kind, J))
        for (j, t), (units, passes) in self.work.items():
            for h in range(GH):
                order.append(("score", j, t, h))
                order += [("unit", J, n) for J, n in with_head(units, h)]
            order += passes
        if steps:
            order.append(("acc", NJ - 1))
        first = 0 if steps else NORM_RING
        banks = NRING - first
        self.bank = {use: first + n % banks for n, use in enumerate(order)}
        self.former = dict(zip(order, [None] * banks + order))

    def prep_count(self, J):
        return 1 + list(self.preps).index(J)

    def stack_count(self, J):
        return self.prep_count(J) if self.steps else 1

    def max_count(self, J):
        return 1 + self.maxima.index(J)


ACC_AT = 1
LEAD = [21, 12, 15, 8, 14, 8, 0, GH * TI * 3]
STOP = [0, 0, 0, 0, 0, 0, 2, 0]
NEXT_MAX_AT = 19
WITHIN = {J: (J - 3, {3: 0, 4: 5, 5: 4, 6: 2, 7: 3}[J]) for J in range(3, NJ)}
START_ORDER = [("qk", NEXT), ("stat", 3), ("qk", NEXT + 1), ("norm", 3), ("qk", NEXT + 2), ("stat", 4), ("norm", 4),
               ("v", NEXT), ("stat", 5), ("norm", 5), ("v", NEXT + 1), ("stat", 6), ("norm", 6), ("v", NEXT + 2),
               ("stat", 7), ("norm", 7), ("max", NEXT), ("max", NEXT + 1)]
STAGED = 3
STAGING = slice(4 * QB, (4 + STAGED) * QB)
STAGED_HEADS = (1, 2)
START = Plan([], {NEXT: None, NEXT + 1: None, NEXT + 2: None}, [NEXT, NEXT + 1])
GROUP = Plan(range(NJ), {**WITHIN, NEXT: (NJ - 1, 4), NEXT + 1: (NJ - 1, 14), NEXT + 2: (NJ - 1, 22)},
             list(range(2, NEXT + 2)))
LAST = Plan(range(NJ), WITHIN, list(range(2, NJ)))


def block_kernel(nc, x, gamma, beta, wqkv, w1, s1, w2, s2, h1w, h1s, h2w, h2s, w3, s3, out):
    with ExitStack() as ctx:
        def sb(name, shape, dt=fp32):
            return ctx.enter_context(nc.sbuf_tensor(name, shape, dt))

        xres = sb("xres", [P, S // P, E])
        ident = sb("ident", [P, P])
        eps = sb("eps", [P, 1])
        QS = sb("QS", [P, NQ, GH, QB], fp32r)
        early = [QS[:, n, :, :].rearrange("p h q -> p (h q)").rearrange("p (c f) -> p c f", c=w.shape[0] // P)
                 for n, w in enumerate((w1, w2, w3))]
        early_load = [ctx.enter_context(nc.semaphore(f"early_load{n}")) for n in range(3)]
        low_bits = sb("low_bits", [1, 1], int32)
        banks = [ctx.enter_context(nc.psum_tensor(f"bank{i}", [P, 512], fp32)) for i in range(8)]
        with ExitStack() as own:
            def sba(name, shape, dt=fp32):
                return own.enter_context(nc.sbuf_tensor(name, shape, dt))

            xnT = sba("xnT", [P, EC, S])
            KS = sba("KS", [P, GH, S], fp32r)
            V = sba("V", [P, S // P, GH, VW])
            qscale = sba("qscale", [P, 1])
            mask = sba("mask", [P, P], bf16)
            ident16 = sba("ident16", [P, P], bf16)
            PR = sba("PR", [P, NPB, GH, QB])
            norm = Normaliser(nc, own, xres, ident, eps, xnT, PR, banks)
            norm.begin(nc, x, gamma, beta, V, qscale, mask, ident16)
            attend(nc, norm, PR, wqkv, xres, ident, xnT, KS, QS, V, qscale, mask, ident16, banks,
                   (w1, w2, h1w, h2w, w3), low_bits, tuple(zip(early, (w1, w2, w3), early_load)))
        inexact = nc.values_load(low_bits[0:1, 0:1], min_val=0, max_val=2 ** LOW_BITS - 1)
        with nc.If(inexact == 0):
            nc.all_engine_barrier()
            feed_forward_exact(nc, w1, s1, w2, s2, h1w, h1s, h2w, h2s, w3, s3, out, xres, ident, eps, banks,
                               QS, early, early_load)
        with nc.Else():
            nc.all_engine_barrier()
            feed_forward(nc, w1, s1, w2, s2, h1w, h1s, h2w, h2s, w3, s3, out, xres, ident, eps, banks)


def clear(nc, sems):
    for s in sems:
        nc.gpsimd.sem_clear(s)
    nc.all_engine_barrier()


class Normaliser:

    FIRST = 3

    def __init__(self, nc, ctx, xres, ident, eps, xnT, PR, banks):
        def sem(name):
            return ctx.enter_context(nc.semaphore(name))

        def sb(name, shape, dt=fp32):
            return ctx.enter_context(nc.sbuf_tensor(name, shape, dt))

        self.xres, self.ident, self.eps, self.xnT, self.banks = xres, ident, eps, xnT, banks
        self.xn = PR[:, 0, :, :].rearrange("p h q -> p (h q)").rearrange("p (s i e) -> p s i e", s=2, i=TI)
        self.gb = sb("gb", [P, 2, EC])
        self.stats = sb("stats", [P, TI, 6])
        self.mv = sb("mv", [P, TI, 2])
        self.std = sb("std", [P, TI, 1])
        self.rstd = sb("rstd", [P, TI, 1])
        self.const_load = sem("const_load")
        self.x_load = [sem(f"x_load{c}") for c in range(NJ)]
        self.zeroed = sem("zeroed")
        self.consts = sem("consts")
        self.cast_done = sem("cast_done")
        self.filled = sem("filled")
        self.stat_done = sem("stat_done")
        self.std_done = sem("std_done")
        self.rstd_done = sem("rstd_done")
        self.xn_done = sem("xn_done")
        self.xnt_ready = sem("xnt_ready")
        self.xnt_done = sem("xnt_done")

    def statistics(self, dve, c):
        dve.wait_ge(self.x_load[c], 16)
        for i in range(TI):
            dve.bn_stats(self.stats[:, i, :], self.xres[:, TI * c + i, :]).then_inc(self.stat_done, 1)
        dve.wait_ge(self.stat_done, 2 * TI * c + TI)
        for i in range(TI):
            dve.bn_aggr(self.mv[:, i, :], self.stats[:, i, :]).then_inc(self.stat_done, 1)

    def scale(self, dve, c):
        dve.wait_ge(self.std_done, c + 1)
        dve.reciprocal(self.rstd[:, :, :], self.std[:, :, :]).then_inc(self.rstd_done, 1)
        dve.wait_ge(self.rstd_done, c + 1)
        if c >= 2:
            dve.wait_ge(self.xnt_ready, EC * (c - 1))
        for i in range(TI):
            dve.tensor_scalar(self.xn[:, c % 2, i, :], self.xres[:, TI * c + i, :], self.mv[:, i, 0:1],
                              self.rstd[:, i, :], ALU.subtract, ALU.mult).then_inc(self.xn_done, 1)

    def deviation(self, act, c):
        act.wait_ge(self.stat_done, 2 * TI * (c + 1))
        act.activation(self.std[:, :, :], self.mv[:, :, 1:2], ACT.Sqrt, bias=self.eps[:, :]).then_inc(self.std_done, 1)

    def bank(self, c, f):
        return self.banks[(EC * c + f) % NORM_RING]

    def transpose(self, pe, c):
        pe.wait_ge(self.xn_done, TI * (c + 1))
        for f in range(EC):
            if EC * c + f >= NORM_RING:
                pe.wait_ge(self.xnt_done, EC * c + f - NORM_RING + 1)
            for i in range(TI):
                last = pe.transpose(self.bank(c, f)[:, P * i:P * (i + 1)],
                                    self.xn[:, c % 2, i, P * f:P * (f + 1)], self.ident[:, :])
            last.then_inc(self.xnt_ready, 1)

    def copy(self, act, c):
        for f in range(EC):
            act.wait_ge(self.xnt_ready, EC * c + f + 1)
            act.activation(self.xnT[:, f, QB * c:QB * (c + 1)], self.bank(c, f)[:, :], ACT.Identity,
                           scale=self.gb[:, 0, f:f + 1], bias=self.gb[:, 1, f:f + 1]).then_inc(self.xnt_done, 1)

    def fill(self, pool, KS, QS, stacked, staging, staged_heads):
        pool.memset(QS[ROWS:P, :, :, :].bitcast(fp32), 0.0).then_inc(self.filled, 1)
        parts = [KS[ROWS:P, h:h + 1, :] for h in range(GH) if h not in staged_heads]
        parts += [KS[ROWS:P, h:h + 1, 0:staging.start] for h in staged_heads]
        parts += [KS[ROWS:P, h:h + 1, staging.stop:S] for h in staged_heads]
        for n, part in enumerate(parts):
            pool.wait_ge(self.filled, n + 1)
            pool.memset(part.bitcast(fp32), 1.0).then_inc(self.filled, 1)
        pool.wait_ge(stacked, 16 * 32)
        for n, h in enumerate(staged_heads):
            pool.wait_ge(self.filled, len(parts) + n + 1)
            pool.memset(KS[ROWS:P, h:h + 1, staging].bitcast(fp32), 1.0).then_inc(self.filled, 1)

    def begin(self, nc, x, gamma, beta, V, qscale, mask, ident16):
        ident, eps, zeroed, consts = self.ident, self.eps, self.zeroed, self.consts
        with ExitStack() as ctx:
            block = ctx.enter_context(nc.Block())

            @block.sync
            def _(sp):
                sp.dma_start(self.gb[:, 0, :], gamma).then_inc(self.const_load, 16)
                sp.dma_start(self.gb[:, 1, :], beta).then_inc(self.const_load, 16)
                for c in range(NJ):
                    sp.dma_start(self.xres[:, TI * c:TI * (c + 1), :],
                                 x[0, QB * c:QB * (c + 1), :].rearrange("(t p) e -> p t e", p=P))\
                      .then_inc(self.x_load[c], 16)

            @block.gpsimd
            def _(pool):
                pool.memset(ident[:, :], 0.0).then_inc(zeroed, 1)
                pool.memset(mask[:, :], 0.0).then_inc(zeroed, 1)
                pool.memset(eps[:, :], EPS).then_inc(consts, 1)
                pool.memset(qscale[:, :], float(D) ** -0.5).then_inc(zeroed, 1)
                pool.wait_ge(zeroed, 3)
                pool.affine_select(out=ident[:, :], in_=ident[:, :], compare_op=ALU.not_equal, fill=1.0, base=0,
                                   pattern=[[-1, P]], channel_multiplier=1).then_inc(consts, 1)
                pool.affine_select(out=mask[:, :], in_=mask[:, :], compare_op=ALU.is_ge, fill=MASK, base=0,
                                   pattern=[[-1, P]], channel_multiplier=1).then_inc(consts, 1)
                pool.affine_select(out=qscale[:, :], in_=qscale[:, :], compare_op=ALU.is_gt, fill=1.0, base=GE,
                                   pattern=[[0, 1]], channel_multiplier=-1).then_inc(consts, 1)
                pool.memset(V[:, :, :, :], 0.0).then_inc(zeroed, 1)
                pool.wait_ge(zeroed, 4)
                pool.memset(V[:, :, :, D:D + 1], 1.0).then_inc(consts, 1)

            @block.scalar
            def _(act):
                act.wait_ge(self.const_load, 32)
                act.wait_ge(consts, 1)
                self.deviation(act, 0)
                for c in range(self.FIRST):
                    if c < self.FIRST - 1:
                        self.deviation(act, c + 1)
                    self.copy(act, c)

            @block.vector
            def _(dve):
                for c in range(self.FIRST):
                    self.statistics(dve, c)
                    self.scale(dve, c)
                dve.wait_ge(consts, 2)
                dve.tensor_copy(ident16[:, :], ident[:, :]).then_inc(self.cast_done, 1)

            @block.tensor
            def _(pe):
                pe.wait_ge(consts, 2)
                for c in range(self.FIRST):
                    self.transpose(pe, c)


def attend(nc, norm, PR, wqkv, xres, ident, xnT, KS, QS, V, qscale, mask, ident16, banks, ff_weights, low_bits, early):
    with ExitStack() as ctx:
        sems = []

        def sem(name):
            sems.append(ctx.enter_context(nc.semaphore(name)))
            return sems[-1]

        def sb(name, shape, dt=fp32):
            return ctx.enter_context(nc.sbuf_tensor(name, shape, dt))

        wg = sb("wg", [P, EC, 3 * GE])
        qk_hi = sb("qk_hi", [P, QB], fp32r)
        qk_lo = sb("qk_lo", [P, QB], fp32r)
        acc_sb = sb("acc_sb", [P, QB])
        pm = sb("pm", [P, GH * TI, NJ])
        rowmax = sb("rowmax", [P, GH * TI])
        mneg = sb("mneg", [P, 2, GH * TI], fp32r)
        mrow = sb("mrow", [2 * GH * TI, P], fp32r)
        recip = sb("recip", [P, TI, GH, 1])
        attn = sb("attn", [P, TI, GH, D])
        low_row = sb("low_row", [1, P])
        low_part = sb("low_part", [P, 1])
        low_max = sb("low_max", [P, 1], int32)
        chunks = [xnT[:, 0, WC * slot:WC * (slot + 1)].bitcast(int32) for slot in range(2)]
        ored = xnT[:, 1, 0:WC].bitcast(int32)

        RING, ACC = banks[0:NRING], banks[NRING]

        wg_load = sem("wg_load")
        qk_ready = sem("qk_ready")
        hi_done = sem("hi_done")
        lo_done = sem("lo_done")
        stacked = sem("stacked")
        v_ready = sem("v_ready")
        v_done = sem("v_done")
        mx_ready = sem("mx_ready")
        mx_done = sem("mx_done")
        rowmax_done = sem("rowmax_done")
        mneg_hi = sem("mneg_hi")
        mneg_done = sem("mneg_done")
        mt_ready = sem("mt_ready")
        mrow_done = sem("mrow_done")
        max_stacked = sem("max_stacked")
        st_ready = sem("st_ready")
        exp_done = sem("exp_done")
        av_done = sem("av_done")
        acc_done = sem("acc_done")
        at_ready = sem("at_ready")
        recip_done = sem("recip_done")
        attn_done = sem("attn_done")
        res_done = sem("res_done")
        first_chunk = sem("first_chunk")
        chunk_load = [sem(f"chunk_load{i}") for i in range(2)]
        or_done = sem("or_done")
        row_load = sem("row_load")

        def st_count(j, t, h):
            return GH * (TBASE[j] + t) + h + 1

        def staged(plan, J, head, part):
            at = STAGING.start + QB * (J - NEXT)
            return part[:, :] if plan.steps else KS[:, head, at:at + QB]

        def hi_part(plan, J):
            return staged(plan, J, STAGED_HEADS[0], qk_hi)

        def lo_part(plan, J):
            return staged(plan, J, STAGED_HEADS[1], qk_lo)

        def ring_bank(plan, *use):
            return RING[plan.bank[use]]

        def tile_count(j, t):
            return TBASE[j] + t + 1

        def weight_chunks():
            for w in ff_weights:
                r = WC // w.shape[1]
                for at in range(0, w.shape[0], P * r):
                    yield w[at:at + P * r, :].rearrange("(p r) f -> p (r f)", r=r).bitcast(int32)

        n_chunks = len(list(weight_chunks()))

        def program(g, plan):
            block = ctx_g.enter_context(nc.Block())

            @block.sync
            def _(sp):
                def load_weights():
                    if NJ - 1 in plan.preps:
                        sp.wait_ge(v_ready, plan.prep_count(NJ - 1))
                    sp.dma_start(wg[:, :, :], wqkv[bass.ds(g + 1, 1), :, :].rearrange("o p (c f) -> p (o c) f", c=EC))\
                      .then_inc(wg_load, 16)

                def stack(j, part, rows_q, rows_k, count=1):
                    for r in rows_q:
                        for h in range(GH):
                            sp.dma_start(QS[r * D:(r + 1) * D, j % NQ:j % NQ + count, h, :].bitcast(fp32),
                                         part[h * D:(h + 1) * D, :].bitcast(fp32)
                                         .rearrange("p (c q) -> p c q", c=count)).then_inc(stacked, 16)
                    for r in rows_k:
                        for h in range(GH):
                            sp.dma_start(KS[r * D:(r + 1) * D, h, QB * j:QB * (j + count)].bitcast(fp32),
                                         part[GE + h * D:GE + (h + 1) * D, :].bitcast(fp32)).then_inc(stacked, 16)

                def stack_block(J):
                    sp.wait_ge(hi_done, plan.prep_count(J))
                    stack(J % NJ, qk_hi, (0, 2), (0, 1))
                    sp.wait_ge(lo_done, plan.prep_count(J))
                    stack(J % NJ, qk_lo, (1, 3), (2, 3))

                def stack_max(J):
                    j = J % NJ
                    sp.wait_ge(mrow_done, plan.max_count(J))
                    for part in range(2):
                        sp.dma_start(QS[MROW + part:MROW + part + 1, j % NQ, :, :].bitcast(fp32),
                                     mrow[part * GH * TI:(part + 1) * GH * TI, :].bitcast(fp32)).then_inc(max_stacked, 16)

                if not plan.steps:
                    load_weights()
                    sp.wait_ge(hi_done, STAGED)
                    stack(0, KS[:, STAGED_HEADS[0], STAGING], (0, 2), (0, 1), STAGED)
                    sp.wait_ge(lo_done, STAGED)
                    stack(0, KS[:, STAGED_HEADS[1], STAGING], (1, 3), (2, 3), STAGED)
                    for J in plan.maxima:
                        stack_max(J)
                for j in plan.steps:
                    for t in range(tiles_of(j)):
                        if (j, t) == (NJ - 3, 0) and NEXT in plan.preps:
                            load_weights()
                        for kind, J in plan.work[j, t][1]:
                            if kind == "qk":
                                stack_block(J)
                            if kind == "max":
                                stack_max(J)
                if plan is LAST:
                    sp.wait_ge(v_ready, plan.prep_count(NJ - 1))
                    for n, chunk in enumerate(weight_chunks()):
                        if n == 0:
                            sp.dma_start(ored, chunk).then_inc(first_chunk, 16)
                            continue
                        if n >= 3:
                            sp.wait_ge(or_done, n - 2)
                        sp.dma_start(chunks[n % 2], chunk).then_inc(chunk_load[n % 2], 16)
                    sp.wait_ge(or_done, n_chunks + 2)
                    sp.dma_start(low_row[:, :], low_part[:, :]).then_inc(row_load, 16)
                if NEXT in plan.preps:
                    sp.wait_ge(wg_load, 16)
                sp.wait_ge(stacked, 16 * 32 * plan.stack_count(list(plan.preps)[-1]))
                sp.wait_ge(max_stacked, 32 * len(plan.maxima))

            @block.gpsimd
            def _(pool):
                if not plan.steps:
                    norm.fill(pool, KS, QS, stacked, STAGING, STAGED_HEADS)
                if plan is LAST:
                    pool.wait_ge(st_ready, st_count(NJ - 1, 0, 0))
                    for dst, w, loaded in early:
                        pool.dma_start(dst, w.rearrange("(c p) f -> p c f", p=P)).then_inc(loaded, 16)
                    for dst, w, loaded in early:
                        pool.wait_ge(loaded, 16)

            @block.scalar
            def _(act):
                def high_part(J):
                    count = plan.prep_count(J)
                    act.wait_ge(qk_ready, count)
                    if plan.steps and count > 1:
                        act.wait_ge(stacked, 16 * 32 * (count - 1))
                    act.activation(hi_part(plan, J), ring_bank(plan, "qk", J)[:, :], ACT.Copy,
                                   scale=qscale[:, :]).then_inc(hi_done, 1)

                def copy_v(J):
                    j, count = J % NJ, plan.prep_count(J)
                    act.wait_ge(v_ready, count)
                    act.activation(V[:, TI * j:TI * (j + 1), :, 0:D],
                                   ring_bank(plan, "v", J)[:, 0:TI * GE].rearrange("p (i h d) -> p i h d", i=TI, h=GH),
                                   ACT.Copy).then_inc(v_done, 1)

                def copy_max(J):
                    count = plan.max_count(J)
                    act.wait_ge(mt_ready, count)
                    if count > 1:
                        act.wait_ge(max_stacked, 32 * (count - 1))
                    act.activation(mrow[:, :], ring_bank(plan, "max", J)[0:2 * GH * TI, 0:P], ACT.Copy)\
                       .then_inc(mrow_done, 1)

                def copy_acc(j):
                    act.wait_ge(av_done, tile_count(j, tiles_of(j) - 1))
                    if j >= 1:
                        act.wait_ge(at_ready, j)
                    act.activation(acc_sb[:, :], ACC[:, :], ACT.Copy).then_inc(acc_done, 1)

                if not plan.steps:
                    for kind, J in START_ORDER:
                        if kind == "stat":
                            norm.deviation(act, J)
                        if kind == "norm":
                            norm.copy(act, J)
                        if kind == "qk":
                            high_part(J)
                        if kind == "v":
                            copy_v(J)
                        if kind == "max":
                            copy_max(J)
                for j in plan.steps:
                    for t in range(tiles_of(j)):
                        off = max(0, P * (t - TI * j))
                        for h in range(GH):
                            act.wait_ge(st_ready, st_count(j, t, h))
                            if h == 0 and tile_count(j, t) > NPB:
                                act.wait_ge(av_done, tile_count(j, t) - NPB)
                            act.activation(PR[:, t % NPB, h, off:QB], ring_bank(plan, "score", j, t, h)[:, off:QB],
                                           ACT.Exp)\
                               .then_inc(exp_done, 1)
                        if t == 0 and j > 0:
                            copy_acc(j - 1)
                        for kind, J in plan.work[j, t][1]:
                            if kind != "acc":
                                {"qk": high_part, "v": copy_v, "max": copy_max}[kind](J)
                if plan.steps:
                    copy_acc(NJ - 1)

            @block.vector
            def _(dve):
                def split(J):
                    count = plan.prep_count(J)
                    dve.wait_ge(hi_done, count)
                    if plan.steps and count > 1:
                        dve.wait_ge(stacked, 16 * 32 * (count - 1))
                    dve.scalar_tensor_tensor(out=lo_part(plan, J), in0=ring_bank(plan, "qk", J)[:, :],
                                             scalar=qscale[:, :],
                                             in1=hi_part(plan, J).bitcast(fp32), op0=ALU.mult, op1=ALU.subtract)\
                       .then_inc(lo_done, 1)

                def maximum(J, n):
                    h, i, c, width = max_unit(J % NJ, n)
                    v = plan.base[J] + n
                    dve.wait_ge(mx_ready, v + 1)
                    dve.reduce_max(pm[:, h * TI + i, c:c + 1], ring_bank(plan, "unit", J, n)[:, 0:width], AX.X)\
                       .then_inc(mx_done, 1)

                def row_maximum(J):
                    j, count = J % NJ, plan.max_count(J)
                    dve.wait_ge(mx_done, plan.base[J] + units_of(J))
                    dve.tensor_reduce(rowmax[:, :], pm[:, :, 0:j + 1], axis=AX.X, op=ALU.max).then_inc(rowmax_done, 1)
                    dve.wait_ge(rowmax_done, count)
                    if count > 1:
                        dve.wait_ge(mt_ready, count - 1)
                    dve.tensor_scalar(mneg[:, 0, :], rowmax[:, :], -1.0, None, ALU.mult).then_inc(mneg_hi, 1)
                    dve.wait_ge(mneg_hi, count)
                    dve.scalar_tensor_tensor(out=mneg[:, 1, :], in0=rowmax[:, :], scalar=-1.0,
                                             in1=mneg[:, 0, :].bitcast(fp32), op0=ALU.mult, op1=ALU.subtract)\
                       .then_inc(mneg_done, 1)

                def attention_out(j):
                    dve.wait_ge(at_ready, j + 1)
                    sums = ring_bank(plan, "acc", j)[:, :].rearrange("p (i h w) -> p i h w", i=TI, h=GH)
                    dve.reciprocal(recip[:, :, :, :], sums[:, :, :, D:D + 1]).then_inc(recip_done, 1)
                    dve.wait_ge(recip_done, j + 1)
                    dve.tensor_tensor(attn[:, :, :, :], sums[:, :, :, 0:D],
                                      recip[:, :, :, :].broadcast_to([P, TI, GH, D]), ALU.mult).then_inc(attn_done, 1)
                    dve.wait_ge(attn_done, j + 1)
                    own = xres[:, TI * j:TI * (j + 1), bass.ds(g * GE, GE)]
                    dve.tensor_tensor(own, own, attn[:, :, :, :].rearrange("p i h d -> p i (h d)"), ALU.add)\
                       .then_inc(res_done, 1)

                def test_weights():
                    dve.wait_ge(first_chunk, 16)
                    for n in range(1, n_chunks):
                        dve.wait_ge(chunk_load[n % 2], 16 * ((n + 1) // 2))
                        if n >= 2:
                            dve.wait_ge(or_done, n - 1)
                        dve.tensor_tensor(ored, ored, chunks[n % 2], ALU.bitwise_or).then_inc(or_done, 1)
                    dve.wait_ge(or_done, n_chunks - 1)
                    dve.tensor_scalar(ored, ored, 2 ** LOW_BITS - 1, None, ALU.bitwise_and).then_inc(or_done, 1)
                    dve.wait_ge(or_done, n_chunks)
                    dve.tensor_reduce(low_max[:, :], ored, axis=AX.X, op=ALU.max).then_inc(or_done, 1)
                    dve.wait_ge(or_done, n_chunks + 1)
                    dve.tensor_copy(low_part[:, :], low_max[:, :]).then_inc(or_done, 1)
                    dve.wait_ge(row_load, 16)
                    dve.tensor_reduce(low_bits[:, :], low_row[:, :], axis=AX.X, op=ALU.max).then_inc(or_done, 1)
                    dve.wait_ge(or_done, n_chunks + 3)

                if not plan.steps:
                    for kind, J in START_ORDER:
                        if kind == "stat":
                            norm.statistics(dve, J)
                        if kind == "norm":
                            norm.scale(dve, J)
                        if kind == "qk":
                            split(J)
                        if kind == "max":
                            for n in range(units_of(J)):
                                maximum(J, n)
                            row_maximum(J)
                for j in plan.steps:
                    for t in range(tiles_of(j)):
                        units, passes = plan.work[j, t]
                        for J, n in units:
                            maximum(J, n)
                            if n == units_of(J) - 1:
                                row_maximum(J)
                        for kind, J in passes:
                            if kind == "acc":
                                attention_out(J)
                            if kind == "qk":
                                split(J)
                if plan is LAST:
                    test_weights()
                if plan.steps:
                    attention_out(NJ - 1)

            @block.tensor
            def _(pe):
                def ring_free(*use):
                    former = plan.former[use]
                    if former is None:
                        return
                    kind, j = former[0:2]
                    if kind == "score":
                        pe.wait_ge(exp_done, st_count(*former[1:]))
                    if kind == "unit":
                        pe.wait_ge(mx_done, plan.base[j] + former[2] + 1)
                    if kind == "qk":
                        pe.wait_ge(lo_done, plan.prep_count(j))
                    if kind == "v":
                        pe.wait_ge(v_done, plan.prep_count(j))
                    if kind == "max":
                        pe.wait_ge(mrow_done, plan.max_count(j))
                    if kind == "acc":
                        pe.wait_ge(attn_done, j + 1)

                def project_qk(J):
                    j = J % NJ
                    if J == NEXT:
                        pe.wait_ge(wg_load, 16)
                    ring_free("qk", J)
                    for c in range(EC):
                        last = pe.matmul(ring_bank(plan, "qk", J)[:, :], wg[:, c, 0:2 * GE],
                                         xnT[:, c, QB * j:QB * (j + 1)],
                                         start=(c == 0), stop=(c == EC - 1))
                    last.then_inc(qk_ready, 1)

                def project_v(J):
                    j = J % NJ
                    ring_free("v", J)
                    for i in range(TI):
                        at = QB * j + P * i
                        for c in range(EC):
                            last = pe.matmul(ring_bank(plan, "v", J)[:, GE * i:GE * (i + 1)], xnT[:, c, at:at + P],
                                             wg[:, c, 2 * GE:3 * GE], start=(c == 0), stop=(c == EC - 1))
                    last.then_inc(v_ready, 1)

                def maximum(J, n):
                    j = J % NJ
                    h, i, c, width = max_unit(j, n)
                    v = plan.base[J] + n
                    if n == 0 and J in plan.preps:
                        pe.wait_ge(stacked, 16 * 32 * plan.stack_count(J))
                    ring_free("unit", J, n)
                    diagonal = c == j
                    bank = ring_bank(plan, "unit", J, n)
                    last = pe.matmul(bank[:, 0:width], QS[0:MROW, j % NQ, h, P * i:P * (i + 1)],
                                     KS[0:MROW, h, QB * c:QB * c + width], start=True, stop=not diagonal)
                    if diagonal:
                        last = pe.matmul(bank[:, width - P:width], ident16[:, :], mask[:, :],
                                         start=False, stop=True)
                    last.then_inc(mx_ready, 1)

                def transpose_max(J):
                    ring_free("max", J)
                    pe.wait_ge(mneg_done, plan.max_count(J))
                    pe.transpose(ring_bank(plan, "max", J)[0:2 * GH * TI, 0:P],
                                 mneg[:, :, :].rearrange("p a n -> p (a n)").bitcast(fp32),
                                 ident[:, :]).then_inc(mt_ready, 1)

                def score(j, t, h):
                    off = max(0, P * (t - TI * j))
                    if t == 0 and h == 0 and j in plan.maxima:
                        pe.wait_ge(max_stacked, 32 * plan.max_count(j))
                    ring_free("score", j, t, h)
                    bank = ring_bank(plan, "score", j, t, h)
                    diagonal = t >= TI * j
                    last = pe.matmul(bank[:, off:QB], KS[:, h, P * t:P * (t + 1)],
                                     QS[:, j % NQ, h, off:QB], start=True, stop=not diagonal)
                    if diagonal:
                        last = pe.matmul(bank[:, off:off + P], mask[:, :], ident16[:, :],
                                         start=False, stop=True)
                    last.then_inc(st_ready, 1)

                def product(j, t):
                    off = max(0, P * (t - TI * j))
                    if t == 0:
                        if j >= 1:
                            pe.wait_ge(acc_done, j)
                        if j in plan.preps:
                            pe.wait_ge(v_done, plan.prep_count(j))
                    pe.wait_ge(exp_done, st_count(j, t, GH - 1))
                    for h in range(GH):
                        last = pe.matmul(ACC[VW * h:VW * (h + 1), off:QB], V[:, t, h, :], PR[:, t % NPB, h, off:QB],
                                         start=(t == 0), stop=(t == tiles_of(j) - 1))
                    last.then_inc(av_done, 1)

                def transpose_acc(j):
                    ring_free("acc", j)
                    pe.wait_ge(acc_done, j + 1)
                    for i in range(TI):
                        last = pe.transpose(ring_bank(plan, "acc", j)[:, P * i:P * (i + 1)],
                                            acc_sb[:, P * i:P * (i + 1)], ident[:, :])
                    last.then_inc(at_ready, 1)

                if not plan.steps:
                    for kind, J in START_ORDER:
                        if kind == "norm":
                            norm.transpose(pe, J)
                        if kind == "qk":
                            project_qk(J)
                        if kind == "v":
                            project_v(J)
                        if kind == "max":
                            if J == NEXT:
                                pe.wait_ge(norm.filled, 1 + GH + len(STAGED_HEADS))
                            for n in range(units_of(J)):
                                maximum(J, n)
                            transpose_max(J)
                last_tile = None
                for j in plan.steps:
                    for t in range(tiles_of(j)):
                        units, passes = plan.work[j, t]
                        for h in range(GH):
                            score(j, t, h)
                            for J, n in with_head(units, h):
                                maximum(J, n)
                            if h == AV_AFTER and last_tile:
                                product(*last_tile)
                        last_tile = j, t
                        for kind, J in passes:
                            {"qk": project_qk, "v": project_v, "max": transpose_max, "acc": transpose_acc}[kind](J)
                if plan.steps:
                    product(*last_tile)
                    transpose_acc(NJ - 1)

        with ExitStack() as ctx_g:
            program(-1, START)
        clear(nc, sems)
        with nc.Fori(0, G - 1) as g:
            with ExitStack() as ctx_g:
                program(g, GROUP)
            clear(nc, sems)
        with ExitStack() as ctx_g:
            program(G - 1, LAST)


def feed_forward_exact(nc, w1, s1, w2, s2, h1w, h1s, h2w, h2s, w3, s3, out, xres, ident, eps, banks,
                       QS, early, early_load):
    with ExitStack() as ctx:
        sems = []

        def sem(name, kept=False):
            s = ctx.enter_context(nc.semaphore("e_" + name))
            if not kept:
                sems.append(s)
            return s

        def sb(name, shape, dt=fp32):
            return ctx.enter_context(nc.sbuf_tensor("e_" + name, shape, dt))

        NB = 4
        NR, NTMP = 6, 4
        RING, TB = banks[0:NR], banks[6:8]
        UNITS = 3 * FC
        NS = 2 * TI
        NY = 3 * TI

        w1_sb, w2_sb, w3_sb = early
        h1_sb = sb("h1_sb", [P, FC, FF], fp32r)
        h2_sb = sb("h2_sb", [P, FC, FF], fp32r)
        s_sb = sb("s_sb", [P, 4, FC])
        s3_sb = sb("s3_sb", [P, E])
        x1T = QS[:, 3, :, :].rearrange("p (a f) q -> p a f q", a=2)
        hid = sb("hid", [P, 2, 2, FC, QB], fp32r)
        tmp = sb("tmp", [P, NTMP, QB])
        y = sb("y", [P, TI, E])
        stats = sb("stats", [P, TI, 6])
        mv = sb("mv", [P, TI, 2])
        std = sb("std", [P, TI, 1])
        rstd = sb("rstd", [P, TI, 1])
        ystats = sb("y_stats", [P, TI, 6])
        ymv = sb("y_mv", [P, TI, 2])
        ystd = sb("y_std_sb", [P, TI, 1])
        yrstd = sb("y_rstd_sb", [P, TI, 1])

        h_load = [sem(f"h_load{i}", kept=True) for i in range(2)]
        s_load = sem("s_load")
        x1_stat = sem("x1_stat")
        x1_std = sem("x1_std")
        x1_rstd = sem("x1_rstd")
        x1_done = sem("x1_done")
        x1_kept = sem("x1_kept")
        x1t_ready = sem("x1t_ready")
        x1t_hi = sem("x1t_hi")
        x1t_lo = sem("x1t_lo")
        glu_ready = sem("glu_ready")
        silu_done = sem("silu_done")
        glu_done = sem("glu_done")
        hid_ready = sem("hid_ready")
        gelu_done = sem("gelu_done")
        hi_done = sem("hi_done")
        parts_done = sem("parts_done")
        y_ready = sem("y_ready")
        y_done = sem("y_done")
        y_stat = sem("y_stat")
        y_std = sem("y_std")
        y_rstd = sem("y_rstd")
        o_done = sem("o_done")
        stored = sem("stored")

        def unit(T, n):
            return UNITS * T + n

        def program(b):
            block = ctx_b.enter_context(nc.Block())

            @block.sync
            def _(sp):
                for v, s in enumerate((s1, s2, h1s, h2s)):
                    sp.dma_start(s_sb[:, v, :], s).then_inc(s_load, 16)
                sp.dma_start(s3_sb[:, :], s3.rearrange("(o e) -> o e", o=1).broadcast_to([P, E])).then_inc(s_load, 16)
                for T in range(NB):
                    sp.wait_ge(o_done, T + 1)
                    sp.dma_start(out_v[bass.ds(NB * b + T, 1), :, :, :].rearrange("o p t e -> p (o t) e"),
                                 y[:, :, :]).then_inc(stored, 16)
                sp.wait_ge(stored, 16 * NB)

            @block.gpsimd
            def _(pool):
                for dst, w, loaded in ((h1_sb, h1w, h_load[0]), (h2_sb, h2w, h_load[1])):
                    pool.dma_start(dst[:, :, :], w.rearrange("(c p) f -> p c f", p=P)).then_inc(loaded, 16)

            @block.scalar
            def _(act):
                def std_x1(T):
                    act.wait_ge(x1_stat, NS * (T + 1))
                    act.activation(std[:, :, :], mv[:, :, 1:2], ACT.Sqrt, bias=eps[:, :]).then_inc(x1_std, 1)

                def std_y(T):
                    act.wait_ge(y_stat, NY * (T + 1))
                    act.activation(ystd[:, :, :], ymv[:, :, 1:2], ACT.Sqrt, bias=eps[:, :]).then_inc(y_std, 1)

                def copy_x1T(T):
                    for f in range(EC):
                        act.wait_ge(x1t_ready, EC * T + f + 1)
                        act.activation(x1T[:, 0, f, :], TB[f][:, :], ACT.Copy).then_inc(x1t_hi, 1)

                def gated_hi(T, o):
                    act.wait_ge(glu_done, FC * T + o + 1)
                    act.activation(hid[:, T % 2, 0, o, :], tmp[:, unit(T, o) % NTMP, :], ACT.Copy).then_inc(hi_done, 1)

                def tmp_free(u):
                    if u >= NTMP:
                        act.wait_ge(parts_done, u - NTMP + 1)

                std_x1(0)
                copy_x1T(0)
                act.wait_ge(s_load, 16 * 5)
                for T in range(NB):
                    for o in range(FC):
                        act.wait_ge(glu_ready, FC * T + o + 1)
                        tmp_free(unit(T, o))
                        act.activation(tmp[:, unit(T, o) % NTMP, :], RING[2 * (o % 3)][:, :], ACT.Silu,
                                       scale=s_sb[:, 0, o:o + 1]).then_inc(silu_done, 1)
                        if o > 0:
                            gated_hi(T, o - 1)
                    gated_hi(T, FC - 1)
                    for n in range(2 * FC):
                        u = unit(T, FC + n)
                        act.wait_ge(hid_ready, 2 * FC * T + n + 1)
                        tmp_free(u)
                        act.activation(tmp[:, u % NTMP, :], RING[(4 + n) % NR][:, :], ACT.Gelu,
                                       scale=s_sb[:, 2 + n // FC, n % FC:n % FC + 1]).then_inc(gelu_done, 1)
                        if n == 4:
                            if T > 0:
                                std_y(T - 1)
                            if T < NB - 1:
                                std_x1(T + 1)
                    if T < NB - 1:
                        copy_x1T(T + 1)
                std_y(NB - 1)

            @block.vector
            def _(dve):
                def tokens(T):
                    return [xres[:, bass.ds(TI * NB * b + TI * T + i, 1), :].rearrange("p o e -> p (o e)")
                            for i in range(TI)]

                def x1_statistics(T):
                    for i in range(TI):
                        dve.bn_stats(stats[:, i, :], tokens(T)[i]).then_inc(x1_stat, 1)
                    dve.wait_ge(x1_stat, NS * T + TI)
                    for i in range(TI):
                        dve.bn_aggr(mv[:, i, :], stats[:, i, :]).then_inc(x1_stat, 1)

                def x1_normalise(T):
                    dve.wait_ge(x1_std, T + 1)
                    if T >= 2:
                        dve.wait_ge(stored, 16 * (T - 1))
                    dve.reciprocal(rstd[:, :, :], std[:, :, :]).then_inc(x1_rstd, 1)
                    dve.wait_ge(x1_rstd, T + 1)
                    for i in range(TI):
                        dve.tensor_scalar(y[:, i, :], tokens(T)[i], mv[:, i, 0:1], rstd[:, i, :],
                                          ALU.subtract, ALU.mult).then_inc(x1_done, 1)
                    for i in range(TI):
                        own = tokens(T)[i]
                        dve.tensor_scalar(own, own, mv[:, i, 0:1], rstd[:, i, :],
                                          ALU.subtract, ALU.mult).then_inc(x1_kept, 1)

                def x1T_low(T):
                    for f in range(EC):
                        dve.wait_ge(x1t_hi, EC * T + f + 1)
                        dve.tensor_tensor(x1T[:, 1, f, :], TB[f][:, :], x1T[:, 0, f, :].bitcast(fp32), ALU.subtract)\
                           .then_inc(x1t_lo, 1)

                def low_part(u, buffer, c):
                    dve.wait_ge(hi_done, u + 1)
                    dve.tensor_tensor(hid[:, buffer, 1, c, :], tmp[:, u % NTMP, :],
                                      hid[:, buffer, 0, c, :].bitcast(fp32), ALU.subtract).then_inc(parts_done, 1)

                def y_read(T):
                    if T > 0:
                        dve.wait_ge(stored, 16 * T)
                    for i in range(TI):
                        dve.wait_ge(y_ready, TI * T + i + 1)
                        dve.tensor_tensor(y[:, i, :], RING[2 + i][:, 0:E], s3_sb[:, :], ALU.mult).then_inc(y_done, 1)

                def y_statistics(T):
                    for i in range(TI):
                        dve.wait_ge(y_done, TI * T + i + 1)
                        dve.wait_ge(x1_kept, TI * T + i + 1)
                        dve.tensor_tensor(y[:, i, :], y[:, i, :], tokens(T)[i], ALU.add).then_inc(y_stat, 1)
                    for i in range(TI):
                        dve.wait_ge(y_stat, NY * T + i + 1)
                        dve.bn_stats(ystats[:, i, :], y[:, i, :]).then_inc(y_stat, 1)
                    dve.wait_ge(y_stat, NY * T + 2 * TI)
                    for i in range(TI):
                        dve.bn_aggr(ymv[:, i, :], ystats[:, i, :]).then_inc(y_stat, 1)

                def y_normalise(T):
                    dve.wait_ge(y_std, T + 1)
                    dve.reciprocal(yrstd[:, :, :], ystd[:, :, :]).then_inc(y_rstd, 1)
                    dve.wait_ge(y_rstd, T + 1)
                    for i in range(TI):
                        last = dve.tensor_scalar(y[:, i, :], y[:, i, :], ymv[:, i, 0:1], yrstd[:, i, :],
                                                 ALU.subtract, ALU.mult)
                    last.then_inc(o_done, 1)

                def y_last():
                    T = NB - 1
                    dve.wait_ge(stored, 16 * T)
                    for i in range(TI):
                        dve.wait_ge(y_ready, TI * T + i + 1)
                        dve.tensor_tensor(y[:, i, :], RING[2 + i][:, 0:E], s3_sb[:, :], ALU.mult).then_inc(y_done, 1)
                        dve.wait_ge(y_done, TI * T + i + 1)
                        dve.wait_ge(x1_kept, TI * T + i + 1)
                        dve.tensor_tensor(y[:, i, :], y[:, i, :], tokens(T)[i], ALU.add).then_inc(y_stat, 1)
                        dve.wait_ge(y_stat, NY * T + 3 * i + 1)
                        dve.bn_stats(ystats[:, i, :], y[:, i, :]).then_inc(y_stat, 1)
                        dve.wait_ge(y_stat, NY * T + 3 * i + 2)
                        dve.bn_aggr(ymv[:, i, :], ystats[:, i, :]).then_inc(y_stat, 1)

                x1_statistics(0)
                x1_normalise(0)
                x1T_low(0)
                dve.wait_ge(s_load, 16 * 5)
                for T in range(NB):
                    if T > 0:
                        y_read(T - 1)
                    for o in range(FC):
                        u = unit(T, o)
                        dve.wait_ge(silu_done, FC * T + o + 1)
                        dve.scalar_tensor_tensor(out=tmp[:, u % NTMP, :], in0=RING[2 * (o % 3) + 1][:, :],
                                                 scalar=s_sb[:, 1, o:o + 1], in1=tmp[:, u % NTMP, :],
                                                 op0=ALU.mult, op1=ALU.mult).then_inc(glu_done, 1)
                        if o > 0:
                            low_part(u - 1, T % 2, o - 1)
                    low_part(unit(T, FC - 1), T % 2, FC - 1)
                    if T > 0:
                        y_statistics(T - 1)
                    for n in range(2 * FC):
                        u = unit(T, FC + n)
                        buffer = (T + 1 + n // FC) % 2
                        dve.wait_ge(gelu_done, 2 * FC * T + n + 1)
                        dve.tensor_copy(hid[:, buffer, 0, n % FC, :], tmp[:, u % NTMP, :]).then_inc(hi_done, 1)
                        low_part(u, buffer, n % FC)
                        if n == 2 and T < NB - 1:
                            x1_statistics(T + 1)
                        if n == 5 and T > 0:
                            y_normalise(T - 1)
                        if n == 9 and T < NB - 1:
                            x1_normalise(T + 1)
                    if T < NB - 1:
                        x1T_low(T + 1)
                y_last()
                y_normalise(NB - 1)

            @block.tensor
            def _(pe):
                def transpose_x1(T):
                    pe.wait_ge(x1_done, TI * (T + 1))
                    for f in range(EC):
                        for i in range(TI):
                            last = pe.transpose(TB[f][:, P * i:P * (i + 1)], y[:, i, P * f:P * (f + 1)], ident[:, :])
                        last.then_inc(x1t_ready, 1)

                transpose_x1(0)
                for loaded in early_load:
                    pe.wait_ge(loaded, 16)
                for T in range(NB):
                    for o in range(FC):
                        if T > 0 and o in (1, 2):
                            pe.wait_ge(y_done, TI * (T - 1) + 2 * o)
                        if o >= 3:
                            pe.wait_ge(glu_done, FC * T + o - 2)
                        for w, at in ((w1_sb, 0), (w2_sb, 1)):
                            for c in range(EC):
                                if o == 0 and at == 0:
                                    pe.wait_ge(x1t_lo, EC * T + c + 1)
                                for part in range(2):
                                    last = pe.matmul(RING[2 * (o % 3) + at][:, :], w[:, c, P * o:P * (o + 1)],
                                                     x1T[:, part, c, :], start=(c == 0 and part == 0),
                                                     stop=(c == EC - 1 and part == 1))
                        last.then_inc(glu_ready, 1)
                    for n in range(2 * FC):
                        layer, o = divmod(n, FC)
                        w = (h1_sb, h2_sb)[layer]
                        if n == 0:
                            pe.wait_ge(glu_done, FC * T + NR)
                        if T == 0 and o == 0:
                            pe.wait_ge(h_load[layer], 16 * b + 16)
                        if n >= NR:
                            pe.wait_ge(gelu_done, 2 * FC * T + n - NR + 1)
                        for c in range(FC):
                            if o == 0:
                                pe.wait_ge(parts_done, unit(T, FC * layer) + c + 1)
                            for part in range(2):
                                last = pe.matmul(RING[(4 + n) % NR][:, :], w[:, c, P * o:P * (o + 1)],
                                                 hid[:, (T + layer) % 2, part, c, :], start=(c == 0 and part == 0),
                                                 stop=(c == FC - 1 and part == 1))
                        last.then_inc(hid_ready, 1)
                    if T < NB - 1:
                        transpose_x1(T + 1)
                    pe.wait_ge(gelu_done, 2 * FC * T + FC + TI + 2)
                    order = [(i, c) for c in range(FC) for i in range(TI)]
                    if T == NB - 1:
                        order = sorted(order)
                    for i, c in order:
                        if i == 0:
                            pe.wait_ge(parts_done, unit(T, 2 * FC) + c + 1)
                        for part in range(2):
                            last = pe.matmul(RING[2 + i][:, 0:E], hid[:, T % 2, part, c, P * i:P * (i + 1)],
                                             w3_sb[:, c, :], start=(c == 0 and part == 0),
                                             stop=(c == FC - 1 and part == 1))
                        if c == FC - 1:
                            last.then_inc(y_ready, 1)

        out_v = out.rearrange("o (b t p) e -> b p (o t) e", p=P, t=TI)
        with nc.Fori(0, NJ // NB) as b:
            with ExitStack() as ctx_b:
                program(b)
            clear(nc, sems)


def feed_forward(nc, w1, s1, w2, s2, h1w, h1s, h2w, h2s, w3, s3, out, xres, ident, eps, banks):
    with ExitStack() as ctx:
        sems = []

        def sem(name, kept=False):
            s = ctx.enter_context(nc.semaphore(name))
            if not kept:
                sems.append(s)
            return s

        def sb(name, shape, dt=fp32):
            return ctx.enter_context(nc.sbuf_tensor(name, shape, dt))

        NB = 1
        w1_sb = sb("w1_sb", [P, EC, FF])
        w2_sb = sb("w2_sb", [P, EC, FF])
        h1_sb = sb("h1_sb", [P, FC, FF])
        h2_sb = sb("h2_sb", [P, FC, FF])
        w3_sb = sb("w3_sb", [P, FC, E])
        s_sb = sb("s_sb", [P, 4, FC])
        s3_sb = sb("s3_sb", [P, E])
        x1 = sb("x1", [P, NB, TI, E])
        x1T = sb("x1T", [P, NB, EC, QB])
        hid = sb("hid", [P, 2, FC, QB])
        gate = sb("gate", [P, 2, QB])
        stats = sb("ff_stats", [P, TI, 6])
        mv = sb("ff_mv", [P, TI, 2])
        std = sb("ff_std", [P, TI, 1])
        rstd = sb("ff_rstd", [P, TI, 1])
        ystats = sb("y_stats", [P, TI, 6])
        ymv = sb("y_mv", [P, TI, 2])
        ystd = sb("y_std_sb", [P, TI, 1])
        yrstd = sb("y_rstd_sb", [P, TI, 1])
        y = sb("y", [P, NB, TI, E])
        o_sb = sb("o_sb", [P, NB, TI, E])

        NR = 6
        RING, TB = banks[0:NR], banks[6:8]
        NS, NY = 2 * TI, 3 * TI

        w_load = [sem(f"w_load{i}", kept=True) for i in range(5)]
        s_load = sem("s_load", kept=True)
        x1_stat = sem("x1_stat")
        x1_std = sem("x1_std")
        x1_rstd = sem("x1_rstd")
        y_std = sem("y_std")
        y_rstd = sem("y_rstd")
        x1_done = sem("x1_done")
        x1t_ready = sem("x1t_ready")
        x1t_done = sem("x1t_done")
        glu_ready = sem("glu_ready")
        silu_done = sem("silu_done")
        glu_done = sem("glu_done")
        hid_ready = sem("hid_ready")
        gelu_done = sem("gelu_done")
        y_ready = sem("y_ready")
        y_done = sem("y_done")
        y_stat = sem("y_stat")
        o_done = sem("o_done")
        stored = sem("stored")

        def program(b):
            block = ctx_b.enter_context(nc.Block())

            @block.sync
            def _(sp):
                for T in range(NB):
                    sp.wait_ge(o_done, T + 1)
                    sp.dma_start(out_v[bass.ds(NB * b + T, 1), :, :, :].rearrange("o p t e -> p (o t) e"),
                                 o_sb[:, T, :, :]).then_inc(stored, 16)
                sp.wait_ge(stored, 16 * NB)

            @block.scalar
            def _(act):
                def copy_x1T(T):
                    for f in range(EC):
                        act.wait_ge(x1t_ready, EC * T + f + 1)
                        act.activation(x1T[:, T, f, :], TB[f][:, :], ACT.Copy).then_inc(x1t_done, 1)

                def std_x1(T):
                    act.wait_ge(x1_stat, NS * (T + 1))
                    act.activation(std[:, :, :], mv[:, :, 1:2], ACT.Sqrt, bias=eps[:, :]).then_inc(x1_std, 1)

                def std_y(T):
                    act.wait_ge(y_stat, NY * (T + 1))
                    act.activation(ystd[:, :, :], ymv[:, :, 1:2], ACT.Sqrt, bias=eps[:, :]).then_inc(y_std, 1)

                std_x1(0)
                copy_x1T(0)
                for T in range(NB):
                    for o in range(FC):
                        n = FC * T + o
                        act.wait_ge(glu_ready, n + 1)
                        if n >= 2:
                            act.wait_ge(glu_done, n - 1)
                        act.activation(gate[:, n % 2, :], RING[2 * (o % 3)][:, :], ACT.Silu,
                                       scale=s_sb[:, 0, o:o + 1]).then_inc(silu_done, 1)
                    if T > 0:
                        std_y(T - 1)
                    if T < NB - 1:
                        std_x1(T + 1)
                    for layer in range(2):
                        for o in range(FC):
                            n = FC * layer + o
                            act.wait_ge(hid_ready, 2 * FC * T + n + 1)
                            act.activation(hid[:, (layer + 1) % 2, o, :], RING[(4 + n) % NR][:, :], ACT.Gelu,
                                           scale=s_sb[:, 2 + layer, o:o + 1]).then_inc(gelu_done, 1)
                    if T < NB - 1:
                        copy_x1T(T + 1)
                std_y(NB - 1)

            @block.vector
            def _(dve):
                def layernorm_x1(T):
                    tok = [xres[:, bass.ds(NB * TI * b + TI * T + i, 1), :].rearrange("p o e -> p (o e)")
                           for i in range(TI)]
                    for i in range(TI):
                        dve.bn_stats(stats[:, i, :], tok[i]).then_inc(x1_stat, 1)
                    dve.wait_ge(x1_stat, NS * T + TI)
                    for i in range(TI):
                        dve.bn_aggr(mv[:, i, :], stats[:, i, :]).then_inc(x1_stat, 1)
                    dve.wait_ge(x1_std, T + 1)
                    dve.reciprocal(rstd[:, :, :], std[:, :, :]).then_inc(x1_rstd, 1)
                    dve.wait_ge(x1_rstd, T + 1)
                    for i in range(TI):
                        dve.tensor_scalar(x1[:, T, i, :], tok[i], mv[:, i, 0:1], rstd[:, i, :],
                                          ALU.subtract, ALU.mult).then_inc(x1_done, 1)

                def gated(T):
                    for o in range(FC):
                        n = FC * T + o
                        dve.wait_ge(silu_done, n + 1)
                        dve.scalar_tensor_tensor(out=hid[:, 0, o, :], in0=RING[2 * (o % 3) + 1][:, :],
                                                 scalar=s_sb[:, 1, o:o + 1], in1=gate[:, n % 2, :],
                                                 op0=ALU.mult, op1=ALU.mult).then_inc(glu_done, 1)

                def residual(T):
                    for i in range(TI):
                        dve.wait_ge(y_ready, TI * T + i + 1)
                        dve.tensor_tensor(y[:, T, i, :], RING[2 + i][:, 0:E], s3_sb[:, :], ALU.mult).then_inc(y_done, 1)
                    for i in range(TI):
                        dve.wait_ge(y_done, TI * T + i + 1)
                        dve.tensor_tensor(y[:, T, i, :], y[:, T, i, :], x1[:, T, i, :], ALU.add).then_inc(y_stat, 1)
                    for i in range(TI):
                        dve.wait_ge(y_stat, NY * T + i + 1)
                        dve.bn_stats(ystats[:, i, :], y[:, T, i, :]).then_inc(y_stat, 1)
                    dve.wait_ge(y_stat, NY * T + 2 * TI)
                    for i in range(TI):
                        dve.bn_aggr(ymv[:, i, :], ystats[:, i, :]).then_inc(y_stat, 1)

                def output(T):
                    dve.wait_ge(y_std, T + 1)
                    dve.reciprocal(yrstd[:, :, :], ystd[:, :, :]).then_inc(y_rstd, 1)
                    dve.wait_ge(y_rstd, T + 1)
                    for i in range(TI):
                        last = dve.tensor_scalar(o_sb[:, T, i, :], y[:, T, i, :], ymv[:, i, 0:1], yrstd[:, i, :],
                                                 ALU.subtract, ALU.mult)
                    last.then_inc(o_done, 1)

                layernorm_x1(0)
                for T in range(NB):
                    gated(T)
                    if T > 0:
                        output(T - 1)
                    if T < NB - 1:
                        layernorm_x1(T + 1)
                    residual(T)
                output(NB - 1)

            @block.tensor
            def _(pe):
                def transpose_x1(T):
                    pe.wait_ge(x1_done, TI * (T + 1))
                    for f in range(EC):
                        for i in range(TI):
                            last = pe.transpose(TB[f][:, P * i:P * (i + 1)], x1[:, T, i, P * f:P * (f + 1)],
                                                ident[:, :])
                        last.then_inc(x1t_ready, 1)

                transpose_x1(0)
                for T in range(NB):
                    pe.wait_ge(x1t_done, EC * (T + 1))
                    for o in range(FC):
                        if T > 0 and o in (1, 2):
                            pe.wait_ge(y_done, TI * (T - 1) + 2 * o)
                        if o >= 3:
                            pe.wait_ge(glu_done, FC * T + o - 2)
                        for w, at in ((w1_sb, 0), (w2_sb, 1)):
                            for c in range(EC):
                                last = pe.matmul(RING[2 * (o % 3) + at][:, :], w[:, c, P * o:P * (o + 1)],
                                                 x1T[:, T, c, :], start=(c == 0), stop=(c == EC - 1))
                        last.then_inc(glu_ready, 1)
                    for layer in range(2):
                        w = (h1_sb, h2_sb)[layer]
                        for o in range(FC):
                            n = FC * layer + o
                            if n >= NR:
                                pe.wait_ge(gelu_done, 2 * FC * T + n - NR + 1)
                            for c in range(FC):
                                if layer == 0 and o == 0:
                                    pe.wait_ge(glu_done, FC * T + max(c, NR - 1) + 1)
                                if layer == 1 and o == 0:
                                    pe.wait_ge(gelu_done, 2 * FC * T + c + 1)
                                last = pe.matmul(RING[(4 + n) % NR][:, :], w[:, c, P * o:P * (o + 1)],
                                                 hid[:, layer, c, :], start=(c == 0), stop=(c == FC - 1))
                            last.then_inc(hid_ready, 1)
                    if T < NB - 1:
                        transpose_x1(T + 1)
                    for i in range(TI):
                        for c in range(FC):
                            if i == 0:
                                pe.wait_ge(gelu_done, 2 * FC * T + FC + max(c, TI + 1) + 1)
                            last = pe.matmul(RING[2 + i][:, 0:E], hid[:, 0, c, P * i:P * (i + 1)], w3_sb[:, c, :],
                                             start=(c == 0), stop=(c == FC - 1))
                        last.then_inc(y_ready, 1)

        with ExitStack() as ctx_l:
            block = ctx_l.enter_context(nc.Block())

            @block.sync
            def _(sp):
                for v, s in enumerate((s1, s2, h1s, h2s)):
                    sp.dma_start(s_sb[:, v, :], s).then_inc(s_load, 16)
                sp.dma_start(s3_sb[:, :], s3.rearrange("(o e) -> o e", o=1).broadcast_to([P, E])).then_inc(s_load, 16)
                for n, (dst, src) in enumerate(((w1_sb, w1), (w2_sb, w2), (h1_sb, h1w), (h2_sb, h2w), (w3_sb, w3))):
                    sp.dma_start(dst[:, :, :], src.rearrange("(c p) f -> p c f", p=P)).then_inc(w_load[n], 16)
                sp.wait_ge(s_load, 16 * 5)
                for n in range(5):
                    sp.wait_ge(w_load[n], 16)

        out_v = out.rearrange("o (b t p) e -> b p (o t) e", p=P, t=TI)
        with nc.Fori(0, NJ // NB) as b:
            with ExitStack() as ctx_b:
                program(b)
            clear(nc, sems)


_OUTS = [((1, S, E), "float32")]


def kernel(**inputs):
    import numpy as _np
    import concourse.bacc as _bacc
    from concourse import mybir as _mybir
    from concourse.bass_utils import run_bass_kernel_spmd as _run

    w = _np.asarray(inputs["L0_attn_w_qkv"]).reshape(3, G, GE, EC, P)
    wqkv = _np.ascontiguousarray(w.transpose(1, 4, 3, 0, 2).reshape(G, P, EC * 3 * GE))

    def by_chunk(v):
        return _np.asarray(v).reshape(-1, P).T

    laid = {
        "x": inputs["L0_attn_x"], "gamma": by_chunk(inputs["L0_attn_gamma"]),
        "beta": by_chunk(inputs["L0_attn_beta"]), "wqkv": wqkv,
        "w1": _np.asarray(inputs["L0_ffn_w1_w"]).T, "s1": by_chunk(inputs["L0_ffn_w1_s"]),
        "w2": _np.asarray(inputs["L0_ffn_w2_w"]).T, "s2": by_chunk(inputs["L0_ffn_w2_s"]),
        "h1": _np.asarray(inputs["L0_ffn_h1_w"]).T, "h1s": by_chunk(inputs["L0_ffn_h1_s"]),
        "h2": _np.asarray(inputs["L0_ffn_h2_w"]).T, "h2s": by_chunk(inputs["L0_ffn_h2_s"]),
        "w3": _np.asarray(inputs["L0_ffn_w3_w"]).T, "s3": inputs["L0_ffn_w3_s"],
    }
    nc = _bacc.Bacc("TRN2", target_bir_lowering=False, num_devices=1)
    arrays, args = {}, []
    for name, a in laid.items():
        a = _np.ascontiguousarray(a)
        arrays[f"in_{name}_dram"] = a
        args.append(nc.dram_tensor(f"in_{name}_dram", a.shape, _mybir.dt.from_np(a.dtype), kind="ExternalInput").ap())
    for i, (shape, dtype) in enumerate(_OUTS):
        args.append(nc.dram_tensor(f"out_{i}_dram", shape, _mybir.dt.from_np(_np.dtype(dtype)), kind="ExternalOutput").ap())
    block_kernel(nc, *args)
    r = _run(nc, [arrays], core_ids=[0])
    return r.results[0]["out_0_dram"]
```
